# Optimizing a Trainium2 kernel written in Bass

```python
import numpy as np
import jax
import jax.numpy as jnp

def _softmax(x, axis=-1):
    return jax.nn.softmax(x, axis=axis)

def _gelu(x):
    return jax.nn.gelu(x, approximate=True)

def _silu(x):
    return jax.nn.silu(x)

def _sigmoid(x):
    return jax.nn.sigmoid(x)

def _layernorm(x, axis=-1, eps=1e-05):
    m = jnp.mean(x, axis=axis, keepdims=True)
    v = jnp.var(x, axis=axis, keepdims=True)
    return (x - m) / jnp.sqrt(v + eps)

def _scatter_add(tgt, idx, src, axis=0):
    return tgt.at[idx].add(src)

def _segment_sum(src, seg, n):
    return jax.ops.segment_sum(src, seg, n)
kernel_name = 'mk_recurrent_d1_jaxref_r8_e8dd9a'

def setup_inputs(seed: int=0):
    np.random.seed(seed)
    _w = jnp.asarray

    def _L0_attn_setup():
        import jax, jax.numpy as jnp
        import numpy as np
        N_EMBD = 128
        N_ATTN = 128
        N_HEAD = 16
        N_LAYER = 12
        LAYER_ID = 5
        CTX = 256
        BATCH = 8
        HEAD_SIZE = N_ATTN // N_HEAD
        K_CLAMP = 60.0
        K_EPS = 1e-16

        def _time_decay_init():
            first = 1
            f1 = 3.0 + (LAYER_ID - first) / (N_LAYER - 1 - first) * (1.2 - 3.0)
            f2 = 0.65 + (LAYER_ID - first) / (N_LAYER - 1 - first) * (0.4 - 0.65)
            if LAYER_ID == first:
                f1 += 0.5
            if LAYER_ID == N_LAYER - 2:
                f2 = 0.4
            if LAYER_ID == N_LAYER - 1:
                f2 = 0.37
            h = np.arange(N_HEAD, dtype=np.float64)
            decay_speed = np.power(f2, h / (N_HEAD - 1) * 7) * f1
            return np.log(decay_speed).astype(np.float32)[:, None]
        key = jax.random.key(seed)
        ks = jax.random.split(key, 5)
        x = jax.random.normal(ks[0], (BATCH, CTX, N_EMBD), dtype=jnp.float32)
        tm = np.ones((1, 1, N_EMBD), dtype=np.float32)
        tm[0, 0, :N_EMBD // 2] = 0.0
        scale = 0.02
        return {'x': x, 'time_decay': jnp.asarray(_time_decay_init()), 'time_first': jnp.full((N_HEAD, 1), np.log(0.3), dtype=jnp.float32), 'time_mix': jnp.asarray(tm), 'Wk': jax.random.normal(ks[1], (N_ATTN, N_EMBD), dtype=jnp.float32) * scale, 'Wv': jax.random.normal(ks[2], (N_ATTN, N_EMBD), dtype=jnp.float32) * scale, 'Wr': jax.random.normal(ks[3], (N_ATTN, N_EMBD), dtype=jnp.float32) * scale, 'Wo': jax.random.normal(ks[4], (N_EMBD, N_ATTN), dtype=jnp.float32) * scale}
    _L0_attn_in = _L0_attn_setup()

    def _L0_ffn_setup():
        import jax, jax.numpy as jnp
        import numpy as np
        B, T, D, H, E = (4, 256, 128, 512, 8)
        key = jax.random.key(seed)
        ks = jax.random.split(key, 7)
        x = jax.random.normal(ks[0], (B, T, D), dtype=jnp.float32)
        Wg = jax.random.normal(ks[1], (D, E), dtype=jnp.float32) / np.sqrt(D)
        bg = jax.random.normal(ks[2], (E,), dtype=jnp.float32) * 0.01
        W1 = jax.random.normal(ks[3], (E, D, H), dtype=jnp.float32) / np.sqrt(D)
        b1 = jax.random.normal(ks[4], (E, H), dtype=jnp.float32) * 0.01
        W2 = jax.random.normal(ks[5], (E, H, D), dtype=jnp.float32) / np.sqrt(H)
        b2 = jax.random.normal(ks[6], (E, D), dtype=jnp.float32) * 0.01
        return {'x': x, 'Wg': Wg, 'bg': bg, 'W1': W1, 'b1': b1, 'W2': W2, 'b2': b2}
    _L0_ffn_in = _L0_ffn_setup()
    _d = {'L0_attn_x': _L0_attn_in['x'], 'L0_attn_time_decay': _L0_attn_in['time_decay'], 'L0_attn_time_first': _L0_attn_in['time_first'], 'L0_attn_time_mix': _L0_attn_in['time_mix'], 'L0_attn_Wk': _L0_attn_in['Wk'], 'L0_attn_Wv': _L0_attn_in['Wv'], 'L0_attn_Wr': _L0_attn_in['Wr'], 'L0_attn_Wo': _L0_attn_in['Wo'], 'L0_ffn_Wg': _L0_ffn_in['Wg'], 'L0_ffn_bg': _L0_ffn_in['bg'], 'L0_ffn_W1': _L0_ffn_in['W1'], 'L0_ffn_b1': _L0_ffn_in['b1'], 'L0_ffn_W2': _L0_ffn_in['W2'], 'L0_ffn_b2': _L0_ffn_in['b2']}
    _x0 = _d['L0_attn_x']
    _d['L0_attn_x'] = jax.random.normal(jax.random.fold_in(jax.random.key(seed), 1), (2, 2048, 128), dtype=_x0.dtype)
    del _x0
    return _d

def reference(L0_attn_x, L0_attn_time_decay, L0_attn_time_first, L0_attn_time_mix, L0_attn_Wk, L0_attn_Wv, L0_attn_Wr, L0_attn_Wo, L0_ffn_Wg, L0_ffn_bg, L0_ffn_W1, L0_ffn_b1, L0_ffn_W2, L0_ffn_b2):

    def _L0_attn_ref(x, time_decay, time_first, time_mix, Wk, Wv, Wr, Wo):
        import jax, jax.numpy as jnp
        import numpy as np
        N_EMBD = 128
        N_ATTN = 128
        N_HEAD = 16
        N_LAYER = 12
        LAYER_ID = 5
        CTX = 256
        BATCH = 8
        HEAD_SIZE = N_ATTN // N_HEAD
        K_CLAMP = 60.0
        K_EPS = 1e-16

        def _time_decay_init():
            first = 1
            f1 = 3.0 + (LAYER_ID - first) / (N_LAYER - 1 - first) * (1.2 - 3.0)
            f2 = 0.65 + (LAYER_ID - first) / (N_LAYER - 1 - first) * (0.4 - 0.65)
            if LAYER_ID == first:
                f1 += 0.5
            if LAYER_ID == N_LAYER - 2:
                f2 = 0.4
            if LAYER_ID == N_LAYER - 1:
                f2 = 0.37
            h = np.arange(N_HEAD, dtype=np.float64)
            decay_speed = np.power(f2, h / (N_HEAD - 1) * 7) * f1
            return np.log(decay_speed).astype(np.float32)[:, None]
        B, T, C = x.shape
        H = time_decay.shape[0]
        D = Wk.shape[0] // H
        xs = jnp.pad(x, ((0, 0), (1, 0), (0, 0)))[:, :T]
        xm = x * time_mix + xs * (1.0 - time_mix)
        k = jnp.exp(jnp.minimum(xm @ Wk.T, K_CLAMP))
        v = xm @ Wv.T
        r = xm @ Wr.T
        kv = k * v
        lag = jnp.arange(T)[:, None] - jnp.arange(T)[None, :]
        dec = jnp.exp(time_decay[:, 0])[:, None, None]
        e = jnp.exp(-dec * jnp.maximum(lag - 1, 0).astype(jnp.float32))
        Wm = jnp.where(lag >= 1, e, 0.0)
        Wm = jnp.where(lag == 0, jnp.exp(time_first[:, 0])[:, None, None], Wm)
        kh = k.reshape(B, T, H, D)
        kvh = kv.reshape(B, T, H, D)
        wkv = jnp.einsum('htu,buhd->bthd', Wm, kvh).reshape(B, T, H * D)
        sum_k = jnp.einsum('htu,buhd->bthd', Wm, kh).reshape(B, T, H * D) + K_EPS
        rwkv = jax.nn.sigmoid(r) * wkv / sum_k
        return rwkv @ Wo.T

    def _L0_ffn_ref(x, Wg, bg, W1, b1, W2, b2):
        import jax, jax.numpy as jnp
        import numpy as np
        B, T, D, H, E = (4, 256, 128, 512, 8)
        gate_scores = x @ Wg + bg
        top1 = jnp.argmax(gate_scores, axis=-1)
        onehot = jax.nn.one_hot(top1, Wg.shape[-1], dtype=x.dtype)
        h = jax.nn.relu(jnp.einsum('btd,edh->beth', x, W1) + b1[None, :, None, :])
        y = jnp.einsum('beth,ehd->betd', h, W2) + b2[None, :, None, :]
        out = jnp.einsum('betd,bte->btd', y, onehot)
        return out
    x = L0_attn_x
    xn = _layernorm(x, axis=-1)
    s = _L0_attn_ref(xn, L0_attn_time_decay, L0_attn_time_first, L0_attn_time_mix, L0_attn_Wk, L0_attn_Wv, L0_attn_Wr, L0_attn_Wo)
    g = _silu(_L0_ffn_ref(xn, L0_ffn_Wg, L0_ffn_bg, L0_ffn_W1, L0_ffn_b1, L0_ffn_W2, L0_ffn_b2))
    x = x + s * g
    return x

_drawn_inputs = setup_inputs


def setup_inputs(seed=0):
    import zlib

    import numpy as np

    out = dict(_drawn_inputs(seed))
    spreads = {'L0_attn_time_first': (-1.2039728164672852, 0.6)}
    factors = {'L0_attn_time_decay': 8.0,
     'L0_attn_time_mix': 8.0,
     'L0_attn_Wk': 8.0,
     'L0_attn_Wv': 8.0,
     'L0_attn_Wr': 8.0,
     'L0_attn_Wo': 8.0,
     'L0_ffn_Wg': 8.0,
     'L0_ffn_bg': 8.0,
     'L0_ffn_W1': 8.0,
     'L0_ffn_b1': 44.604,
     'L0_ffn_W2': 8.0,
     'L0_ffn_b2': 200.0}
    for name, (base, spread) in spreads.items():
        noise = np.random.default_rng([zlib.crc32(name.encode()), seed]).standard_normal(out[name].shape)
        drawn = base * np.exp(spread * noise) if base else spread * noise
        out[name] = jnp.asarray(drawn.astype(out[name].dtype))
    for name, factor in factors.items():
        out[name] = (out[name] * factor).astype(out[name].dtype)
    return out
```

```python
from contextlib import ExitStack

import concourse.bass as bass
from concourse import mybir

F32 = mybir.dt.float32
BF16 = mybir.dt.bfloat16
F16 = mybir.dt.float16
I32 = mybir.dt.int32
ALU = mybir.AluOpType
ACT = mybir.ActivationFunctionType
AX = mybir.AxisListType

P = 128
BATCH, T = 2, 2048
TOK = BATCH * T
NT = TOK // P
BLK = 512
TPB = BLK // P
NB = TOK // BLK
NBB = NB // BATCH
HEADS = 16
HEAD = P // HEADS
E = 8
HID = 512
HC = HID // P
RING = 4
NS = -(-(NT + E - 1) // RING) * RING
TURNS = NS // RING
SPARE = NS * P
STAT = 6
LN_EPS = 1e-5
K_EPS = 1e-16
K_CLAMP = 60.0
TAYLOR = 9
SMALL_DECAY = 0.5
Y0 = E * HID


class Steps:

    def __init__(self, eng, sem):
        self.eng, self.sem, self.n = eng, sem, 0

    def link(self, ins):
        ins.then_inc(self.sem, 1)
        self.n = self.n + 1
        self.eng.wait_ge(self.sem, self.n)


def mixture_kernel(nc, x, time_decay, time_first, time_mix, Wk, Wv, Wr, Wo, Wg, bg, W1, b1, W2, b2, out):
    ctx = ExitStack()
    with ctx:
        def sb(name, shape, dt=F32):
            return ctx.enter_context(nc.sbuf_tensor(name, shape, dt))

        def bank(name):
            return ctx.enter_context(nc.psum_tensor(name, [P, BLK], F32))

        def sem(name):
            return ctx.enter_context(nc.semaphore(name))

        xn_rows = nc.dram_tensor("xn_rows", [TOK, P], F32).ap()
        g_rows = nc.dram_tensor("g_rows", [TOK + SPARE, P], F32).ap()

        x_sb = sb("x_sb", [P, NT, P])
        xn_sb = sb("xn_sb", [P, NT, P])
        s_sb = xn_sb
        xnT = sb("xnT", [P, BATCH, T + 1])
        xmT = sb("xmT", [P, TOK])
        kT = sb("kT", [P, TOK])
        vT = sb("vT", [P, TOK])
        rT = sb("rT", [P, TOK])
        g_sb = kT[:, :].rearrange("p (n d) -> p n d", d=P)
        w1 = sb("w1", [P, E, HID])
        w2 = sb("w2", [P, E * HC, P])
        wnat = sb("wnat", [P, 4, P])
        wT = sb("wT", [P, 4, P])
        wg = sb("wg", [P, E])
        bgb = sb("bgb", [P, E])
        bias_nat = sb("bias_nat", [P, (E * HID + E * P) // P])
        bias_r = sb("bias_r", [P, 2, (E * HID + E * P) // P])
        bias_part = sb("bias_part", [P, 3, (E * HID + E * P) // P], BF16)
        bias_row = sb("bias_row", [3, E * HID + E * P], BF16)
        tmix = sb("tmix", [P, 1])
        omt = sb("omt", [P, 1])
        tdec = sb("tdec", [P, 1])
        tfir = sb("tfir", [P, 1])
        dec = sb("dec", [P, 1])
        small = sb("small", [P, 1])
        large = sb("large", [P, 1])
        ydec = sb("ydec", [P, 1])
        minus_over_n = sb("minus_over_n", [P, TAYLOR])
        ytab = sb("ytab", [P, TAYLOR])
        ser = sb("ser", [P, 1])
        a_exp = sb("a_exp", [P, 1])
        a = sb("a", [P, 1])
        ef = sb("ef", [P, 1])
        ident = sb("ident", [P, P])
        upper = sb("upper", [P, P], BF16)
        ones = sb("ones", [P, P], BF16)
        keep = sb("keep", [P, NB])
        stats = sb("stats", [P, NT, STAT])
        msum = sb("msum", [P, NT])
        mdif = sb("mdif", [P, NT])
        var = sb("var", [P, NT])
        std = sb("std", [P, NT])
        rstd = sb("rstd", [P, NT])
        newt = sb("newt", [P, NT])
        nbias = sb("nbias", [P, NT])
        logit = sb("logit", [P, NT, E])
        lmax = sb("lmax", [P, NT])
        first = sb("first", [P, E])
        wsel = sb("wsel", [P, NT, E])
        wmax = sb("wmax", [P, NT])
        oh = sb("oh", [P, E, NT], BF16)
        going = sb("going", [P, E, NT])
        tot = sb("tot", [P, E, NT])
        incl = sb("incl", [P, E, NT])
        excl = sb("excl", [P, E, NT])
        cnt_i = sb("cnt_i", [P, 2, E], I32)
        tiles_f = sb("tiles_f", [P, E])
        one8 = sb("one8", [P, E])
        end_t = sb("end_t", [P, E])
        base_s = sb("base_s", [P, E])
        posw = sb("posw", [P, E, NT])
        pos = sb("pos", [P, NT])
        pos_i = sb("pos_i", [P, 3, NT], I32)
        hi_f = sb("hi_f", [P, NT])
        lo_f = sb("lo_f", [P, NT])
        iota_s = sb("iota_s", [P, NS])
        padrow = sb("padrow", [P, NS])
        iota_h = sb("iota_h", [P, P], F16)
        tokc = sb("tokc", [P, NT])
        ohlo = sb("ohlo", [P, NT, P], F16)
        ohhi = sb("ohhi", [P, 2, NT, NS], F16)
        inv = sb("inv", [P, 2, NS])
        gidx_f = sb("gidx_f", [P, NS])
        pad_f = sb("pad_f", [P, 2, NS])
        gidx = sb("gidx", [P, NS], I32)
        sidx = sb("sidx", [P, NS], I32)
        ecmp = sb("ecmp", [P, NS, E])
        esum = sb("esum", [P, NS])
        etab = sb("etab", [P, NS], I32)
        gi = sb("gi", [P, RING], I32)
        si = sb("si", [P, RING], I32)
        xg = [sb(f"xg{j}", [P, P]) for j in range(RING)]
        xgT = [sb(f"xgT{j}", [P, P]) for j in range(RING)]
        hidT = [sb(f"hidT{j}", [P, HID]) for j in range(2)]
        sgm = [sb(f"sgm{j}", [P, P]) for j in range(2)]
        gout = [sb(f"gout{j}", [P, P]) for j in range(RING)]
        zk = sb("zk", [P, BLK + 1])
        zkv = sb("zkv", [P, BLK + 1])
        ohhi_f = ohhi[:, :, :, :].rearrange("p a n s -> p (a n s)").bitcast(F32)
        hid = [ohhi_f[:, m * HID:(m + 1) * HID] for m in range(2)]
        rw = sb("rw", [P, BLK])
        ohlo_f = ohlo[:, :, :].rearrange("p n s -> p (n s)").bitcast(F32)
        den, rden, num, ratio = (ohlo_f[:, m * BLK:(m + 1) * BLK] for m in range(4))

        psX, psH0, psH1, psT0, psT1, psY, psS, psG = [bank(f"ps{i}") for i in range(8)]
        psH, psT = [psH0, psH1], [psT0, psT1]

        ld_x = [sem("ld_x0"), sem("ld_x1")]
        ld_proj = sem("ld_proj")
        ld_small = sem("ld_small")
        ld_w1 = sem("ld_w1")
        ld_w2 = sem("ld_w2")
        bias_rows_in = sem("bias_rows_in")
        consts = sem("consts")
        pool_step = sem("pool_step")
        dve_step = sem("dve_step")
        act_step = sem("act_step")
        bias_split = sem("bias_split")
        dec_ready = sem("dec_ready")
        omt_ready = sem("omt_ready")
        wT_ps = sem("wT_ps")
        wT_ready = sem("wT_ready")
        var_ready = sem("var_ready")
        std_ready = sem("std_ready")
        ln_ready = sem("ln_ready")
        xn_pool = sem("xn_pool")
        xn_dve = sem("xn_dve")
        xn_stored = sem("xn_stored")
        xnT_ps = sem("xnT_ps")
        xnT_ready = sem("xnT_ready")
        mixed_a = sem("mixed_a")
        xm_ready = sem("xm_ready")
        gates = sem("gates")
        oh_ready = sem("oh_ready")
        prefix_ready = sem("prefix_ready")
        onehots = sem("onehots")
        inv_ps = sem("inv_ps")
        idx_ready = sem("idx_ready")
        experts_ready = sem("experts_ready")
        kvr_ps = [sem("k_ps"), sem("v_ps"), sem("r_ps")]
        kvr_out = [sem("k_out"), sem("v_out"), sem("r_out")]
        gidx_staged = sem("gidx_staged")
        sidx_staged = sem("sidx_staged")
        gathered = [sem(f"gathered{j}") for j in range(RING)]
        scattered = [sem(f"scattered{j}") for j in range(RING)]
        xgT_ps = sem("xgT_ps")
        xgT_ready = sem("xgT_ready")
        hid_ps = sem("hid_ps")
        hid_ready = sem("hid_ready")
        hidT_ps = sem("hidT_ps")
        hidT_ready = sem("hidT_ready")
        y_ps = sem("y_ps")
        sgm_ready = sem("sgm_ready")
        g_ready = sem("g_ready")
        sig_ready = sem("sig_ready")
        k_capped = sem("k_capped")
        k_ready = sem("k_ready")
        kv_ready = sem("kv_ready")
        ratio_ready = sem("ratio_ready")
        rw_ready = sem("rw_ready")
        s_ps = sem("s_ps")
        s_ready = sem("s_ready")
        g_loaded = [sem("g_loaded0"), sem("g_loaded1")]
        prod_ready = sem("prod_ready")
        out_pool = sem("out_pool")
        out_dve = sem("out_dve")
        stored = sem("stored")
        NCONST = 14

        x_v = x.rearrange("b (n p) d -> p (b n) d", p=P)
        out_v = out.rearrange("b (n p) d -> p (b n) d", p=P)
        xn_v = xn_rows.rearrange("(n p) d -> p n d", p=P)
        g_v = g_rows[0:TOK, :].rearrange("(n p) d -> p n d", p=P)
        HALF = NT // 2
        block = ctx.enter_context(nc.Block())

        @block.sync
        def _(sp):
            for b in range(BATCH):
                sp.dma_start(x_sb[:, b * HALF:(b + 1) * HALF, :],
                             x_v[:, b * HALF:(b + 1) * HALF, :]).then_inc(ld_x[b], 16)
            sp.wait_ge(ld_small, 16 * 7)
            sp.wait_ge(ld_proj, 16 * 4)
            sp.dma_start(w1[:, :, :], W1.rearrange("e d h -> d e h")).then_inc(ld_w1, 16)
            sp.dma_start(w2[:, :, :], W2.rearrange("e (c p) d -> p (e c) d", p=P)).then_inc(ld_w2, 16)
            sp.wait_ge(bias_split, 1)
            n1 = E * HID // P
            for j in range(3):
                sp.dma_start(bias_row[j:j + 1, 0:Y0].rearrange("o (p c) -> o p c", c=n1),
                             bias_part[:, j, 0:n1]).then_inc(bias_rows_in, 16)
                sp.dma_start(bias_row[j:j + 1, Y0:].rearrange("o (p c) -> o p c", c=E),
                             bias_part[:, j, n1:]).then_inc(bias_rows_in, 16)
            for b in range(BATCH):
                sp.wait_ge(xn_pool, NBB * (b + 1))
                sp.wait_ge(xn_dve, NBB * (b + 1))
                sp.dma_start(xn_v[:, b * HALF:(b + 1) * HALF, :],
                             xn_sb[:, b * HALF:(b + 1) * HALF, :]).then_inc(xn_stored, 16)
            for j in range(RING):
                sp.wait_ge(scattered[j], 16 * TURNS)
            sp.wait_ge(ratio_ready, NB)
            for b in range(BATCH):
                sp.dma_start(g_sb[:, b * HALF:(b + 1) * HALF, :],
                             g_v[:, b * HALF:(b + 1) * HALF, :]).then_inc(g_loaded[b], 16)
            for c in range(NB):
                if c % 2:
                    sp.wait_ge(out_pool, c // 2 + 1)
                else:
                    sp.wait_ge(out_dve, c // 2 + 1)
                sp.dma_start(out_v[:, c * TPB:(c + 1) * TPB, :],
                             g_sb[:, c * TPB:(c + 1) * TPB, :]).then_inc(stored, 16)
            sp.wait_ge(stored, 16 * NB)

        @block.gpsimd
        def _(pool):
            g = nc.gpsimd
            step = Steps(pool, pool_step)
            step.link(g.memset(ident[:, :], 0.0))
            g.affine_select(out=ident[:, :], in_=ident[:, :], compare_op=ALU.not_equal, fill=1.0, base=0,
                            pattern=[[-1, P]], channel_multiplier=1).then_inc(consts, 1)
            step.link(g.memset(upper[:, :], 1.0))
            g.affine_select(out=upper[:, :], in_=upper[:, :], compare_op=ALU.is_gt, fill=0.0, base=0,
                            pattern=[[1, P]], channel_multiplier=-1).then_inc(consts, 1)
            g.memset(ones[:, :], 1.0).then_inc(consts, 1)
            step.link(g.memset(keep[:, :], 1.0))
            g.memset(keep[:, :].rearrange("p (b k) -> p b k", b=BATCH)[:, :, 0], 0.0).then_inc(consts, 1)
            step.link(g.memset(going[:, :, :], 1.0))
            g.memset(going[:, :, 0], 0.0).then_inc(consts, 1)
            g.memset(one8[:, :], 1.0).then_inc(consts, 1)
            g.memset(xnT[:, :, 0], 0.0).then_inc(consts, 1)
            for n in range(1, TAYLOR + 1):
                last = g.memset(minus_over_n[:, n - 1:n], -1.0 / n)
            last.then_inc(consts, 1)
            g.iota(first[:, :], pattern=[[-1, E]], base=E, channel_multiplier=0,
                   allow_small_or_imprecise_dtypes=True).then_inc(consts, 1)
            g.iota(iota_h[:, :], pattern=[[1, P]], base=0, channel_multiplier=0,
                   allow_small_or_imprecise_dtypes=True).then_inc(consts, 1)
            g.iota(iota_s[:, :], pattern=[[1, NS]], base=0, channel_multiplier=0,
                   allow_small_or_imprecise_dtypes=True).then_inc(consts, 1)
            g.iota(tokc[:, :], pattern=[[P, NT]], base=-TOK // 2, channel_multiplier=1,
                   allow_small_or_imprecise_dtypes=True).then_inc(consts, 1)
            g.iota(padrow[:, :], pattern=[[P, NS]], base=TOK, channel_multiplier=1,
                   allow_small_or_imprecise_dtypes=True).then_inc(consts, 1)
            g.memset(rw[:, 0:1], 0.0).then_inc(rw_ready, 1)
            g.memset(rw[:, 1:2], 0.0).then_inc(s_ps, 1)
            g.memset(rw[:, 2:3], 0.0).then_inc(s_ready, 1)
            g.memset(zk[:, :], 0.0)
            g.memset(zkv[:, :], 0.0).then_inc(consts, 1)

            pool.wait_ge(ln_ready, 1)
            for k in range(NB):
                for j in range(2):
                    n = k * TPB + j
                    last = g.tensor_scalar(xn_sb[:, n, :], x_sb[:, n, :], rstd[:, n:n + 1], nbias[:, n:n + 1],
                                           ALU.mult, ALU.add)
                last.then_inc(xn_pool, 1)
            def gather(s_i, j, count=None):
                g.tensor_copy(gi[:, j:j + 1], gidx[:, bass.ds(s_i * RING + j, 1)]).then_inc(gidx_staged, 1)
                pool.wait_ge(xn_stored, 16 * BATCH)
                pool.wait_ge(gidx_staged, count)
                g.indirect_dma_start(xg[j][:, :], None, xn_rows,
                                     bass.IndirectOffsetOnAxis(gi[:, j:j + 1], 0)).then_inc(gathered[j], 16)

            def scatter(s_i, j):
                count = s_i * RING + (j + 1)
                pool.wait_ge(g_ready, count)
                g.tensor_copy(si[:, j:j + 1], sidx[:, bass.ds(s_i * RING + j, 1)]).then_inc(sidx_staged, 1)
                pool.wait_ge(idx_ready, 1)
                pool.wait_ge(sidx_staged, count)
                g.indirect_dma_start(g_rows, bass.IndirectOffsetOnAxis(si[:, j:j + 1], 0), gout[j][:, :],
                                     None).then_inc(scattered[j], 16)

            pool.wait_ge(idx_ready, 1)
            pool.wait_ge(xn_stored, 16 * BATCH)
            g.tensor_copy(gi[:, :], gidx[:, 0:RING]).then_inc(pool_step, 1)
            pool.wait_ge(pool_step, step.n + 1)
            for j in range(RING):
                g.indirect_dma_start(xg[j][:, :], None, xn_rows,
                                     bass.IndirectOffsetOnAxis(gi[:, j:j + 1], 0)).then_inc(gathered[j], 16)

            def turn(i, scatters, gathers, attend):
                for j in range(RING):
                    if gathers:
                        pool.wait_ge(xgT_ps, i * RING + (j + 1))
                        gather(i + 1, j, count=i * RING + (j + 1))
                    if attend and j == 0:
                        q = i - 1
                        g.tensor_tensor(vT[:, bass.ds(q * BLK, BLK)], kT[:, bass.ds(q * BLK, BLK)],
                                        vT[:, bass.ds(q * BLK, BLK)], ALU.mult).then_inc(kv_ready, 1)
                    if j == RING - 1:
                        scatter(i, 0)
                    elif scatters:
                        scatter(i - 1, j + 1)
                if attend:
                    q = i - 1
                    pool.wait_ge(ratio_ready, i)
                    pool.wait_ge(sig_ready, i)
                    pool.wait_ge(s_ps, i)
                    g.tensor_tensor(rw[:, :], ratio[:, :], rT[:, bass.ds(q * BLK, BLK)],
                                    ALU.mult).then_inc(rw_ready, 1)

            turn(0, False, True, False)
            pool.wait_ge(k_ready, BATCH)
            pool.wait_ge(kvr_out[1], NB)
            with pool.Fori(1, TURNS - 1) as i:
                turn(i, True, True, True)
            turn(TURNS - 1, True, False, False)
            for j in range(1, RING):
                scatter(TURNS - 1, j)
            for c in range(1, NB, 2):
                pool.wait_ge(prod_ready, c + 1)
                g.tensor_tensor(g_sb[:, c * TPB:(c + 1) * TPB, :], g_sb[:, c * TPB:(c + 1) * TPB, :],
                                x_sb[:, c * TPB:(c + 1) * TPB, :], ALU.add).then_inc(out_pool, 1)

        @block.vector
        def _(dve):
            v = nc.vector
            step = Steps(dve, dve_step)
            for b in range(BATCH):
                dve.wait_ge(ld_x[b], 16)
                for n in range(b * HALF, (b + 1) * HALF):
                    last = v.bn_stats(stats[:, n, :], x_sb[:, n, :])
            step.link(last)
            dve.wait_ge(ld_small, 16 * 7)
            dve.wait_ge(consts, NCONST)
            v.tensor_scalar(omt[:, :], tmix[:, :], -1.0, 1.0, ALU.mult, ALU.add).then_inc(omt_ready, 1)
            step.link(v.tensor_copy(bias_part[:, 0, :], bias_nat[:, :]))
            step.link(v.tensor_tensor(bias_r[:, 0, :], bias_nat[:, :], bias_part[:, 0, :], ALU.subtract))
            step.link(v.tensor_copy(bias_part[:, 1, :], bias_r[:, 0, :]))
            step.link(v.tensor_tensor(bias_r[:, 1, :], bias_r[:, 0, :], bias_part[:, 1, :], ALU.subtract))
            v.tensor_copy(bias_part[:, 2, :], bias_r[:, 1, :]).then_inc(bias_split, 1)
            dve.wait_ge(dec_ready, 1)
            step.link(v.tensor_scalar(ydec[:, :], dec[:, :], SMALL_DECAY, None, ALU.min))
            v.tensor_scalar(small[:, :], dec[:, :], SMALL_DECAY, None, ALU.is_le)
            step.link(v.tensor_scalar(ytab[:, :], minus_over_n[:, :], ydec[:, 0:1], None, ALU.mult))
            v.tensor_scalar(large[:, :], small[:, :], -1.0, 1.0, ALU.mult, ALU.add)
            step.link(v.tensor_scalar(ser[:, :], ytab[:, TAYLOR - 1:TAYLOR], 1.0, None, ALU.add))
            for n in range(TAYLOR - 1, 0, -1):
                step.link(v.tensor_scalar(ser[:, :], ser[:, :], ytab[:, n - 1:n], 1.0, ALU.mult, ALU.add))
            step.link(v.tensor_tensor(ser[:, :], ser[:, :], small[:, :], ALU.mult))
            step.link(v.scalar_tensor_tensor(out=a[:, :], in0=a_exp[:, :], scalar=large[:, 0:1],
                                             in1=ser[:, :], op0=ALU.mult, op1=ALU.add))

            v.tensor_tensor(msum[:, :], stats[:, :, 1], stats[:, :, 4], ALU.add)
            step.link(v.tensor_tensor(mdif[:, :], stats[:, :, 1], stats[:, :, 4], ALU.subtract))
            v.tensor_tensor(var[:, :], stats[:, :, 2], stats[:, :, 5], ALU.add)
            step.link(v.scalar_tensor_tensor(out=newt[:, :], in0=mdif[:, :], scalar=0.25, in1=mdif[:, :],
                                             op0=ALU.mult, op1=ALU.mult))
            step.link(v.scalar_tensor_tensor(out=var[:, :], in0=var[:, :], scalar=1.0 / P, in1=newt[:, :],
                                             op0=ALU.mult, op1=ALU.add))
            ins = v.tensor_scalar(var[:, :], var[:, :], LN_EPS, None, ALU.add)
            ins.then_inc(var_ready, 1)
            dve.wait_ge(var_ready, 1)
            dve.wait_ge(std_ready, 1)
            step.link(v.reciprocal(rstd[:, :], std[:, :]))
            step.link(v.tensor_tensor(newt[:, :], rstd[:, :], rstd[:, :], ALU.mult))
            step.link(v.tensor_tensor(newt[:, :], newt[:, :], var[:, :], ALU.mult))
            step.link(v.tensor_scalar(newt[:, :], newt[:, :], -0.5, 1.5, ALU.mult, ALU.add))
            step.link(v.tensor_tensor(rstd[:, :], rstd[:, :], newt[:, :], ALU.mult))
            ins = v.scalar_tensor_tensor(out=nbias[:, :], in0=msum[:, :], scalar=-0.5, in1=rstd[:, :],
                                         op0=ALU.mult, op1=ALU.mult)
            ins.then_inc(ln_ready, 1)
            dve.wait_ge(ln_ready, 1)

            def mix_shifted(k):
                dve.wait_ge(mixed_a, k + 1)
                b, c = divmod(k, NBB)
                if c:
                    dve.wait_ge(xnT_ready, k + 1)
                v.scalar_tensor_tensor(out=xmT[:, k * BLK:(k + 1) * BLK], in0=xnT[:, b, c * BLK:(c + 1) * BLK],
                                       scalar=omt[:, 0:1], in1=xmT[:, k * BLK:(k + 1) * BLK],
                                       op0=ALU.mult, op1=ALU.add).then_inc(xm_ready, 1)

            for k in range(NB):
                for j in range(2, TPB):
                    n = k * TPB + j
                    last = v.tensor_scalar(xn_sb[:, n, :], x_sb[:, n, :], rstd[:, n:n + 1], nbias[:, n:n + 1],
                                           ALU.mult, ALU.add)
                last.then_inc(xn_dve, 1)
                if k >= 2:
                    if k == 2:
                        dve.wait_ge(omt_ready, 1)
                    mix_shifted(k - 2)
            mix_shifted(NB - 2)
            mix_shifted(NB - 1)

            dve.wait_ge(gates, NB)
            gate_ps = psG[:, 0:NT * E].rearrange("p (n e) -> p n e", e=E)
            step.link(v.tensor_tensor(logit[:, :, :], gate_ps, bgb[:, :].unsqueeze(1).to_broadcast([P, NT, E]),
                                      ALU.add))
            step.link(v.tensor_reduce(lmax[:, :], logit[:, :, :], AX.X, ALU.max))
            step.link(v.tensor_tensor(wsel[:, :, :], logit[:, :, :],
                                      lmax[:, :].unsqueeze(2).to_broadcast([P, NT, E]), ALU.is_equal))
            step.link(v.tensor_tensor(wsel[:, :, :], wsel[:, :, :],
                                      first[:, :].unsqueeze(1).to_broadcast([P, NT, E]), ALU.mult))
            step.link(v.tensor_reduce(wmax[:, :], wsel[:, :, :], AX.X, ALU.max))
            ins = v.tensor_tensor(oh[:, :, :].rearrange("p e n -> p n e"), wsel[:, :, :],
                                  wmax[:, :].unsqueeze(2).to_broadcast([P, NT, E]), ALU.is_equal)
            ins.then_inc(oh_ready, 1)
            dve.wait_ge(oh_ready, 1)
            dve.wait_ge(prefix_ready, 1)
            EN = E * NT
            flat = lambda t: t[:, :, :].rearrange("p e n -> p (e n)")
            step.link(v.tensor_copy(flat(tot), psS[:, EN:2 * EN]))
            step.link(v.tensor_tensor_scan(flat(incl), flat(going), flat(tot), 0.0, ALU.mult, ALU.add))
            v.tensor_tensor(flat(excl), flat(incl), flat(tot), ALU.subtract)
            step.link(v.tensor_scalar(cnt_i[:, 0, :], incl[:, :, NT - 1], float(P - 1), None, ALU.add))
            step.link(v.tensor_scalar(cnt_i[:, 1, :], cnt_i[:, 0, :], 7, None, ALU.logical_shift_right))
            step.link(v.tensor_copy(tiles_f[:, :], cnt_i[:, 1, :]))
            step.link(v.tensor_tensor_scan(end_t[:, :], one8[:, :], tiles_f[:, :], 0.0, ALU.mult, ALU.add))
            step.link(v.tensor_tensor(base_s[:, :], end_t[:, :], tiles_f[:, :], ALU.subtract))
            step.link(v.tensor_scalar(base_s[:, :], base_s[:, :], float(P), None, ALU.mult))
            step.link(v.tensor_tensor(flat(posw), psS[:, 0:EN], flat(excl), ALU.add))
            step.link(v.tensor_tensor(posw[:, :, :], posw[:, :, :],
                                      base_s[:, :].unsqueeze(2).to_broadcast([P, E, NT]), ALU.add))
            step.link(v.tensor_tensor(posw[:, :, :], posw[:, :, :], oh[:, :, :], ALU.mult))
            step.link(v.tensor_reduce(pos[:, :], posw[:, :, :].rearrange("p e n -> p n e"), AX.X, ALU.add))
            step.link(v.tensor_copy(pos_i[:, 0, :], pos[:, :]))
            v.tensor_scalar(pos_i[:, 1, :], pos_i[:, 0, :], 7, None, ALU.logical_shift_right)
            step.link(v.tensor_scalar(pos_i[:, 2, :], pos_i[:, 0, :], P - 1, None, ALU.bitwise_and))
            v.tensor_copy(hi_f[:, :], pos_i[:, 1, :])
            step.link(v.tensor_copy(lo_f[:, :], pos_i[:, 2, :]))
            step.link(v.tensor_tensor(ohhi[:, 1, :, :], iota_s[:, :].unsqueeze(1).to_broadcast([P, NT, NS]),
                                      hi_f[:, :].unsqueeze(2).to_broadcast([P, NT, NS]), ALU.is_equal))
            v.tensor_tensor(ohhi[:, 0, :, :], ohhi[:, 1, :, :],
                            tokc[:, :].unsqueeze(2).to_broadcast([P, NT, NS]), ALU.mult)
            for n in range(NT):
                last = v.tensor_scalar(ohlo[:, n, :], iota_h[:, :], lo_f[:, n:n + 1], None, ALU.is_equal)
            last.then_inc(onehots, 1)
            step.link(v.tensor_tensor(ecmp[:, :, :], iota_s[:, :].unsqueeze(2).to_broadcast([P, NS, E]),
                                      end_t[:, :].unsqueeze(1).to_broadcast([P, NS, E]), ALU.is_ge))
            step.link(v.tensor_reduce(esum[:, :], ecmp[:, :, :], AX.X, ALU.add))
            v.tensor_scalar(etab[:, :], esum[:, :], float(E - 1), None, ALU.min).then_inc(experts_ready, 1)
            def cap_keys(b):
                dve.wait_ge(kvr_out[0], NBB * (b + 1))
                v.tensor_scalar(kT[:, b * T:(b + 1) * T], kT[:, b * T:(b + 1) * T], K_CLAMP, None,
                                ALU.min).then_inc(k_capped, 1)

            cap_keys(0)
            dve.wait_ge(inv_ps, 1)
            step.link(v.tensor_copy(inv[:, :, :].rearrange("p a s -> p (a s)"), psG[:, 0:2 * NS]))
            step.link(v.scalar_tensor_tensor(out=gidx_f[:, :], in0=inv[:, 1, :], scalar=float(TOK // 2),
                                             in1=inv[:, 0, :], op0=ALU.mult, op1=ALU.add))
            v.tensor_copy(gidx[:, :], gidx_f[:, :])
            step.link(v.tensor_tensor(pad_f[:, 0, :], inv[:, 1, :], padrow[:, :], ALU.mult))
            step.link(v.tensor_tensor(pad_f[:, 1, :], padrow[:, :], pad_f[:, 0, :], ALU.subtract))
            v.tensor_tensor(sidx[:, :], pad_f[:, 1, :], gidx_f[:, :], ALU.add).then_inc(idx_ready, 1)
            cap_keys(1)

            def gate_rows(i, j):
                dve.wait_ge(sgm_ready, i * RING + (j + 1))
                v.tensor_tensor(gout[j][:, :], psY[:, 0:P], sgm[j % 2][:, :], ALU.mult).then_inc(g_ready, 1)

            def attend(i, part_no):
                q = i - 1
                here = bass.ds(q * BLK, BLK)
                step.n = step0 + q * LOOP_STEPS + done[0]
                before = step.n
                if part_no == 0:
                    v.tensor_scalar(zkv[:, 0:1], zkv[:, BLK:BLK + 1], keep[:, bass.ds(q, 1)], None, ALU.mult)
                    step.link(v.tensor_scalar(zk[:, 0:1], zk[:, BLK:BLK + 1], keep[:, bass.ds(q, 1)], None,
                                              ALU.mult))
                    step.link(v.tensor_tensor_scan(zk[:, 1:BLK + 1], a[:, 0:1].to_broadcast([P, BLK]),
                                                   kT[:, here], zk[:, 0:1], ALU.mult, ALU.add))
                    step.link(v.scalar_tensor_tensor(out=den[:, :], in0=kT[:, here], scalar=ef[:, 0:1],
                                                     in1=zk[:, 0:BLK], op0=ALU.mult, op1=ALU.add))
                    done[0] += 3
                elif part_no == 1:
                    step.link(v.tensor_scalar(den[:, :], den[:, :], K_EPS, None, ALU.add))
                    v.reciprocal(rden[:, 0:BLK // 2], den[:, 0:BLK // 2])
                    done[0] += 1
                elif part_no == 2:
                    step.link(v.reciprocal(rden[:, BLK // 2:BLK], den[:, BLK // 2:BLK]))
                    dve.wait_ge(kv_ready, i)
                    step.link(v.tensor_tensor_scan(zkv[:, 1:BLK + 1], a[:, 0:1].to_broadcast([P, BLK]),
                                                   vT[:, here], zkv[:, 0:1], ALU.mult, ALU.add))
                    done[0] += 2
                else:
                    step.link(v.scalar_tensor_tensor(out=num[:, :], in0=vT[:, here], scalar=ef[:, 0:1],
                                                     in1=zkv[:, 0:BLK], op0=ALU.mult, op1=ALU.add))
                    dve.wait_ge(rw_ready, i)
                    v.tensor_tensor(ratio[:, :], num[:, :], rden[:, :], ALU.mult).then_inc(ratio_ready, 1)
                    done[0] += 1

            LOOP_STEPS = 7
            done = [0]
            step0 = step.n

            def turn(i, first=False, attends=False):
                for j in range(RING):
                    if attends:
                        attend(i, j)
                    if j >= 2 and not first:
                        dve.wait_ge(scattered[j - 2], i * 16)
                    if j >= 2:
                        gate_rows(i, j - 2)
                    elif not first:
                        gate_rows(i - 1, j + 2)

                if not first:
                    for j in range(2, RING):
                        dve.wait_ge(scattered[j], i * 16)

            turn(0, first=True)
            dve.wait_ge(k_ready, BATCH)
            with dve.Fori(1, TURNS - 1) as i:
                turn(i, attends=True)
            assert done[0] == LOOP_STEPS
            turn(TURNS - 1)
            for j in range(2, RING):
                gate_rows(TURNS - 1, j)

            dve.wait_ge(s_ready, NB + 1)
            for c in range(NB):
                if c % NBB == 0:
                    dve.wait_ge(g_loaded[c // NBB], 16)
                cols = slice(c * TPB, (c + 1) * TPB)
                v.tensor_tensor(g_sb[:, cols, :], g_sb[:, cols, :], s_sb[:, cols, :],
                                ALU.mult).then_inc(prod_ready, 1)
                if c % 2 == 0:
                    dve.wait_ge(prod_ready, c + 1)
                    v.tensor_tensor(g_sb[:, cols, :], g_sb[:, cols, :], x_sb[:, cols, :],
                                    ALU.add).then_inc(out_dve, 1)

        @block.scalar
        def _(act):
            s = nc.scalar
            act.dma_start(tmix[:, :], time_mix.rearrange("a b d -> d (a b)")).then_inc(ld_small, 16)
            act.dma_start(bgb[:, :], bg.rearrange("(o e) -> o e", o=1).to_broadcast([P, E])).then_inc(ld_small, 16)
            act.dma_start(wg[:, :], Wg).then_inc(ld_small, 16)
            act.dma_start(bias_nat[:, 0:E * HID // P],
                          b1.rearrange("e h -> (e h)").rearrange("(p c) -> p c", p=P)).then_inc(ld_small, 16)
            act.dma_start(bias_nat[:, E * HID // P:],
                          b2.rearrange("e h -> (e h)").rearrange("(p c) -> p c", p=P)).then_inc(ld_small, 16)
            act.dma_start(tdec[:, :], time_decay.to_broadcast([HEADS, HEAD])).then_inc(ld_small, 16)
            act.dma_start(tfir[:, :], time_first.to_broadcast([HEADS, HEAD])).then_inc(ld_small, 16)
            for t, w in enumerate((Wk, Wv, Wr, Wo)):
                act.dma_start(wnat[:, t, :], w).then_inc(ld_proj, 16)
            act.wait_ge(ld_small, 16 * 7)
            s.activation(dec[:, :], tdec[:, :], ACT.Exp).then_inc(act_step, 1)
            s.activation(ef[:, :], tfir[:, :], ACT.Exp)
            act.wait_ge(act_step, 1)
            s.activation(a_exp[:, :], dec[:, :], ACT.Exp, scale=-1.0).then_inc(dec_ready, 1)
            act.wait_ge(wT_ps, 1)
            s.copy(wT[:, :, :].rearrange("p t d -> p (t d)"), psX[:, :]).then_inc(wT_ready, 1)
            act.wait_ge(var_ready, 1)
            s.activation(std[:, :], var[:, :], ACT.Sqrt).then_inc(std_ready, 1)
            for k in range(NB):
                b, c = divmod(k, NBB)
                act.wait_ge(xnT_ps, k + 1)
                s.copy(xnT[:, b, 1 + c * BLK:1 + (c + 1) * BLK], psT[k % 2][:, :]).then_inc(xnT_ready, 1)
                s.mul(xmT[:, k * BLK:(k + 1) * BLK], psT[k % 2][:, :], tmix[:, 0:1]).then_inc(mixed_a, 1)

            def kvr(k):
                here = bass.ds(k * BLK, BLK)
                for t, (dst, ps) in enumerate(((kT, psH0), (vT, psH1), (rT, psY))):
                    act.wait_ge(kvr_ps[t], k + 1)
                    s.copy(dst[:, here], ps[:, :]).then_inc(kvr_out[t], 1)

            with act.Fori(0, NB) as k:
                kvr(k)

            def exp_k(b):
                act.wait_ge(k_capped, b + 1)
                s.activation(kT[:, b * T:(b + 1) * T], kT[:, b * T:(b + 1) * T], ACT.Exp).then_inc(k_ready, 1)

            def relu(i, j):
                act.wait_ge(hid_ps, i * RING + (j + 1))
                if not isinstance(i, int) or i * RING + j >= 2:
                    act.wait_ge(hidT_ps, i * RING + (j - 1))
                s.activation(hid[j % 2][:, :], psH[j % 2][:, :], ACT.Relu).then_inc(hid_ready, 1)

            def copy_xgT(i, j):
                act.wait_ge(xgT_ps, i * RING + (j + 1))
                if not isinstance(i, int) or i:
                    act.wait_ge(hid_ps, (i - 1) * RING + (j + 1))
                s.copy(xgT[j][:, :], psX[:, 0:P]).then_inc(xgT_ready, 1)

            def copy_hidT(i, j):
                act.wait_ge(hidT_ps, i * RING + (j + 1))
                if not isinstance(i, int) or i * RING + j >= 2:
                    act.wait_ge(y_ps, i * RING + (j - 1))
                s.copy(hidT[j % 2][:, :], psT[j % 2][:, :]).then_inc(hidT_ready, 1)

            def sigmoid_y(i, j):
                act.wait_ge(y_ps, i * RING + (j + 1))
                if not isinstance(i, int) or i * RING + j >= 2:
                    act.wait_ge(g_ready, i * RING + (j - 1))
                s.activation(sgm[j % 2][:, :], psY[:, 0:P], ACT.Sigmoid).then_inc(sgm_ready, 1)

            def turn(i, first=False, last=False, attends=False):
                for j in range(RING):
                    relu(i, j)
                    if j < RING - 1:
                        copy_xgT(i, j + 1)
                    elif not last:
                        copy_xgT(i + 1, 0)
                    if j:
                        copy_hidT(i, j - 1)
                    elif not first:
                        copy_hidT(i - 1, RING - 1)
                    if j >= 2:
                        sigmoid_y(i, j - 2)
                    elif not first:
                        sigmoid_y(i - 1, j + 2)
                    if attends and j == 0:
                        here = bass.ds((i - 1) * BLK, BLK)
                        s.activation(rT[:, here], rT[:, here], ACT.Sigmoid).then_inc(sig_ready, 1)
                if attends:
                    q = i - 1
                    act.wait_ge(s_ps, i + 1)
                    s.copy(s_sb[:, bass.ds(q * TPB, TPB), :], psS[:, :].rearrange("p (n d) -> p n d", d=P)
                           ).then_inc(s_ready, 1)

            for b in range(BATCH):
                exp_k(b)
            copy_xgT(0, 0)
            turn(0, first=True)
            act.wait_ge(kvr_out[2], NB)
            act.wait_ge(xn_stored, 16 * BATCH)
            with act.Fori(1, TURNS - 1) as i:
                turn(i, attends=True)
            turn(TURNS - 1, last=True)
            copy_hidT(TURNS - 1, RING - 1)
            sigmoid_y(TURNS - 1, RING - 2)
            sigmoid_y(TURNS - 1, RING - 1)

        @block.tensor
        def _(pe):
            t = nc.tensor
            pe.wait_ge(consts, NCONST)
            pe.wait_ge(ld_proj, 16 * 4)
            for m in range(4):
                last = t.transpose(psX[:, m * P:(m + 1) * P], wnat[:, m, :], ident[:, :])
            last.then_inc(wT_ps, 1)

            def logits(k):
                b, c = divmod(k, NBB)
                pe.wait_ge(xnT_ready, k + 1)
                for j in range(TPB):
                    n = k * TPB + j
                    c0 = 1 + c * BLK + j * P
                    last = t.matmul(psG[:, n * E:(n + 1) * E], xnT[:, b, c0:c0 + P], wg[:, :],
                                    start=True, stop=True)
                last.then_inc(gates, 1)

            for k in range(NB):
                pe.wait_ge(xn_pool, k + 1)
                pe.wait_ge(xn_dve, k + 1)
                if k >= 2:
                    pe.wait_ge(mixed_a, k - 1)
                for j in range(TPB):
                    last = t.transpose(psT[k % 2][:, j * P:(j + 1) * P], xn_sb[:, k * TPB + j, :], ident[:, :])
                last.then_inc(xnT_ps, 1)
                if k == 1:
                    pe.wait_ge(ld_small, 16 * 7)
                if k:
                    logits(k - 1)
            logits(NB - 1)

            pe.wait_ge(wT_ready, 1)

            def kvr(k, first=False):
                pe.wait_ge(xm_ready, k + 1)
                for m, ps in enumerate((psH0, psH1, psY)):
                    if not first:
                        pe.wait_ge(kvr_out[m], k)
                    t.matmul(ps[:, :], wT[:, m, :], xmT[:, bass.ds(k * BLK, BLK)],
                             start=True, stop=True).then_inc(kvr_ps[m], 1)

            def prefix():
                pe.wait_ge(oh_ready, 1)
                EN = E * NT
                ohf = oh[:, :, :].rearrange("p e n -> p (e n)")
                t.matmul(psS[:, 0:EN], upper[:, :], ohf, start=True, stop=True)
                t.matmul(psS[:, EN:2 * EN], ones[:, :], ohf, start=True, stop=True).then_inc(prefix_ready, 1)

            kvr(0, first=True)
            prefix()
            with pe.Fori(1, NB - 2) as k:
                kvr(k)

            pe.wait_ge(onehots, 1)
            for n in range(NT):
                last = t.matmul(psG[:, 0:2 * NS].rearrange("p (a s) -> p a s", a=2), ohlo[:, n, :],
                                ohhi[:, :, n, :], start=(n == 0), stop=(n == NT - 1))
            last.then_inc(inv_ps, 1)
            for k in range(NB - 2, NB):
                kvr(k)

            def transpose_rows(i, j):
                pe.wait_ge(gathered[j], (i + 1) * 16)
                if not isinstance(i, int) or i * RING + j:
                    pe.wait_ge(xgT_ready, i * RING + j)
                t.transpose(psX[:, 0:P], xg[j][:, :], ident[:, :]).then_inc(xgT_ps, 1)

            def layer1(i, j, e):
                pe.wait_ge(xgT_ready, i * RING + (j + 1))
                if not isinstance(i, int) or i * RING + j >= 2:
                    pe.wait_ge(hid_ready, i * RING + (j - 1))
                t.matmul(psH[j % 2][:, :], xgT[j][:, :], w1[:, bass.ds(e, 1), :].rearrange("p o h -> p (o h)"),
                         start=True, stop=False)
                t.matmul(psH[j % 2][:, :], ones[0:3, :], bias_row[:, bass.ds(e * HID, HID)],
                         start=False, stop=True).then_inc(hid_ps, 1)

            def transpose_hidden(i, j):
                pe.wait_ge(hid_ready, i * RING + (j + 1))
                if not isinstance(i, int) or i * RING + j >= 2:
                    pe.wait_ge(hidT_ready, i * RING + (j - 1))
                for c in range(HC):
                    last = t.transpose(psT[j % 2][:, c * P:(c + 1) * P], hid[j % 2][:, c * P:(c + 1) * P],
                                       ident[:, :])
                last.then_inc(hidT_ps, 1)

            def layer2(i, j, e):
                pe.wait_ge(hidT_ready, i * RING + (j + 1))
                if not isinstance(i, int) or i * RING + j:
                    pe.wait_ge(g_ready, i * RING + j)
                for c in range(HC):
                    t.matmul(psY[:, 0:P], hidT[j % 2][:, c * P:(c + 1) * P],
                             w2[:, bass.ds(e * HC + c, 1), :].rearrange("p o d -> p (o d)"),
                             start=(c == 0), stop=False)
                t.matmul(psY[:, 0:P], ones[0:3, :], bias_row[:, bass.ds(Y0 + e * P, P)],
                         start=False, stop=True).then_inc(y_ps, 1)

            def expert(i, j):
                return pe.value_load(etab[0:1, bass.ds(i * RING + j, 1)], min_val=0, max_val=E - 1)

            def turn(i, first=False, last=False, attends=False):
                for j in range(RING):
                    layer1(i, j, expert(i, j))
                    if j < RING - 1:
                        transpose_rows(i, j + 1)
                    elif not last:
                        transpose_rows(i + 1, 0)
                    if j:
                        transpose_hidden(i, j - 1)
                    elif not first:
                        transpose_hidden(i - 1, RING - 1)
                    if j >= 2:
                        layer2(i, j - 2, expert(i, j - 2))
                    elif not first:
                        layer2(i - 1, j + 2, expert(i - 1, j + 2))
                if attends:
                    q = i - 1
                    pe.wait_ge(rw_ready, i + 1)
                    pe.wait_ge(s_ready, i)
                    for j in range(TPB):
                        out_ins = t.matmul(psS[:, j * P:(j + 1) * P], rw[:, j * P:(j + 1) * P], wT[:, 3, :],
                                           start=True, stop=True)
                    out_ins.then_inc(s_ps, 1)

            pe.wait_ge(experts_ready, 1)
            pe.wait_ge(ld_w1, 16)
            pe.wait_ge(ld_w2, 16)
            pe.wait_ge(bias_rows_in, 16 * 6)
            for m in range(3):
                pe.wait_ge(kvr_out[m], NB)
            transpose_rows(0, 0)
            turn(0, first=True)
            with pe.Fori(1, TURNS - 1) as i:
                turn(i, attends=True)
            turn(TURNS - 1, last=True)
            transpose_hidden(TURNS - 1, RING - 1)
            layer2(TURNS - 1, RING - 2, expert(TURNS - 1, RING - 2))
            layer2(TURNS - 1, RING - 1, expert(TURNS - 1, RING - 1))


_INS = ['L0_attn_x', 'L0_attn_time_decay', 'L0_attn_time_first', 'L0_attn_time_mix', 'L0_attn_Wk', 'L0_attn_Wv',
        'L0_attn_Wr', 'L0_attn_Wo', 'L0_ffn_Wg', 'L0_ffn_bg', 'L0_ffn_W1', 'L0_ffn_b1', 'L0_ffn_W2', 'L0_ffn_b2']


def kernel(**inputs):
    import numpy as _np
    import concourse.bacc as _bacc
    from concourse import mybir as _mybir
    from concourse.bass_utils import run_bass_kernel_spmd as _run

    nc = _bacc.Bacc("TRN2", target_bir_lowering=False, num_devices=1)
    arrays, args = {}, []
    for name in _INS:
        arr = _np.ascontiguousarray(inputs[name])
        arrays[f"in_{name}"] = arr
        args.append(nc.dram_tensor(f"in_{name}", arr.shape, _mybir.dt.from_np(arr.dtype), kind="ExternalInput").ap())
    args.append(nc.dram_tensor("out_x", (BATCH, T, P), F32, kind="ExternalOutput").ap())
    mixture_kernel(nc, *args)
    r = _run(nc, [arrays], core_ids=[0])
    return r.results[0]["out_x"]
```

```python
from contextlib import ExitStack

import concourse.bass as bass
from concourse import mybir

F32 = mybir.dt.float32
BF16 = mybir.dt.bfloat16
F16 = mybir.dt.float16
I32 = mybir.dt.int32
ALU = mybir.AluOpType
ACT = mybir.ActivationFunctionType
AX = mybir.AxisListType

P = 128
BATCH, T = 2, 2048
TOK = BATCH * T
NT = TOK // P
BLK = 512
TPB = BLK // P
NB = TOK // BLK
NBB = NB // BATCH
HEADS = 16
HEAD = P // HEADS
E = 8
HID = 512
HC = HID // P
RING = 4
NS = -(-(NT + E - 1) // RING) * RING
TURNS = NS // RING
SPARE = NS * P
STAT = 6
LN_EPS = 1e-5
K_EPS = 1e-16
K_CLAMP = 60.0
TAYLOR = 9
SMALL_DECAY = 0.5
BR = 3 * E


class Steps:

    def __init__(self, eng, sem):
        self.eng, self.sem, self.n = eng, sem, 0

    def link(self, ins):
        ins.then_inc(self.sem, 1)
        self.n = self.n + 1
        self.eng.wait_ge(self.sem, self.n)


def mixture_kernel(nc, x, time_decay, time_first, time_mix, Wk, Wv, Wr, Wo, Wg, bg, W1, b1, W2, b2, out):
    ctx = ExitStack()
    with ctx:
        def sb(name, shape, dt=F32):
            return ctx.enter_context(nc.sbuf_tensor(name, shape, dt))

        def bank(name):
            return ctx.enter_context(nc.psum_tensor(name, [P, BLK], F32))

        def sem(name):
            return ctx.enter_context(nc.semaphore(name))

        xn_rows = nc.dram_tensor("xn_rows", [TOK, P], F32).ap()
        g_rows = nc.dram_tensor("g_rows", [TOK + SPARE, P], F32).ap()

        x_sb = sb("x_sb", [P, NT, P])
        xn_sb = sb("xn_sb", [P, NT, P])
        s_sb = xn_sb
        xnT = sb("xnT", [P, BATCH, T + 1])
        xmT = sb("xmT", [P, TOK])
        kT = sb("kT", [P, TOK])
        vT = sb("vT", [P, TOK])
        rT = sb("rT", [P, TOK])
        g_sb = kT[:, :].rearrange("p (n d) -> p n d", d=P)
        w1 = sb("w1", [P, E, HID])
        w2 = sb("w2", [P, E * HC, P])
        wnat = sb("wnat", [P, 4, P])
        wT = sb("wT", [P, 4, P])
        wg = sb("wg", [P, E])
        bgb = sb("bgb", [P, E])
        bias_nat = sb("bias_nat", [P, (E * HID + E * P) // P])
        bias_r = sb("bias_r", [P, 2, (E * HID + E * P) // P])
        bias_part = sb("bias_part", [P, 3, (E * HID + E * P) // P], BF16)
        bias_mat = sb("bias_mat", [BR, HID + P], BF16)
        tmix = sb("tmix", [P, 1])
        omt = sb("omt", [P, 1])
        tdec = sb("tdec", [P, 1])
        tfir = sb("tfir", [P, 1])
        dec = sb("dec", [P, 1])
        small = sb("small", [P, 1])
        large = sb("large", [P, 1])
        ydec = sb("ydec", [P, 1])
        minus_over_n = sb("minus_over_n", [P, TAYLOR])
        ytab = sb("ytab", [P, TAYLOR])
        ser = sb("ser", [P, 1])
        a_exp = sb("a_exp", [P, 1])
        a = sb("a", [P, 1])
        ef = sb("ef", [P, 1])
        ident = sb("ident", [P, P])
        upper = sb("upper", [P, P], BF16)
        ones = sb("ones", [P, P], BF16)
        keep = sb("keep", [P, NB])
        stats = sb("stats", [P, NT, STAT])
        msum = sb("msum", [P, NT])
        mdif = sb("mdif", [P, NT])
        var = sb("var", [P, NT])
        std = sb("std", [P, NT])
        rstd = sb("rstd", [P, NT])
        newt = sb("newt", [P, NT])
        nbias = sb("nbias", [P, NT])
        logit = sb("logit", [P, NT, E])
        lmax = sb("lmax", [P, NT])
        first = sb("first", [P, E])
        wsel = sb("wsel", [P, NT, E])
        wmax = sb("wmax", [P, NT])
        oh = sb("oh", [P, E, NT], BF16)
        going = sb("going", [P, E, NT])
        tot = sb("tot", [P, E, NT])
        incl = sb("incl", [P, E, NT])
        excl = sb("excl", [P, E, NT])
        cnt_i = sb("cnt_i", [P, 2, E], I32)
        tiles_f = sb("tiles_f", [P, E])
        one8 = sb("one8", [P, E])
        end_t = sb("end_t", [P, E])
        base_s = sb("base_s", [P, E])
        posw = sb("posw", [P, E, NT])
        pos = sb("pos", [P, NT])
        pos_i = sb("pos_i", [P, 3, NT], I32)
        hi_f = sb("hi_f", [P, NT])
        lo_f = sb("lo_f", [P, NT])
        iota_s = sb("iota_s", [P, NS])
        padrow = sb("padrow", [P, NS])
        iota_h = sb("iota_h", [P, P], F16)
        tokc = sb("tokc", [P, NT])
        ohlo = sb("ohlo", [P, NT, P], F16)
        ohhi = sb("ohhi", [P, 2, NT, NS], F16)
        inv = sb("inv", [P, 2, NS])
        gidx_f = sb("gidx_f", [P, NS])
        pad_f = sb("pad_f", [P, 2, NS])
        gidx = sb("gidx", [P, NS], I32)
        sidx = sb("sidx", [P, NS], I32)
        ecmp = sb("ecmp", [P, NS, E])
        esum = sb("esum", [P, NS])
        etab = sb("etab", [P, NS], I32)
        row_i = sb("row_i", [BR, 2], I32)
        row_e = sb("row_e", [BR, 1])
        sel = sb("sel", [BR, NS], BF16)
        gi = sb("gi", [P, RING], I32)
        si = sb("si", [P, RING], I32)
        xg = [sb(f"xg{j}", [P, P]) for j in range(RING)]
        xgT = [sb(f"xgT{j}", [P, P]) for j in range(2)]
        sel_t = [sb(f"sel_t{j}", [BR, P], BF16) for j in range(RING)]
        w1e = [sb(f"w1e{j}", [P, HID]) for j in range(2)]
        w2e = [sb(f"w2e{j}", [P, HID]) for j in range(2)]
        sgm = [sb(f"sgm{j}", [P, P]) for j in range(2)]
        gout = [sb(f"gout{j}", [P, P]) for j in range(RING)]
        zk = sb("zk", [P, BLK + 1])
        zkv = sb("zkv", [P, BLK + 1])
        ohhi_f = ohhi[:, :, :, :].rearrange("p a n s -> p (a n s)").bitcast(F32)
        hidT = [ohhi_f[:, m * HID:(m + 1) * HID] for m in range(2)]
        rw = sb("rw", [P, BLK])
        ohlo_f = ohlo[:, :, :].rearrange("p n s -> p (n s)").bitcast(F32)
        den, rden, num, signum = (ohlo_f[:, m * BLK:(m + 1) * BLK] for m in range(4))

        psX, psH0, psH1, psT0, psT1, psY, psS, psG = [bank(f"ps{i}") for i in range(8)]
        psH, psT = [psH0, psH1], [psT0, psT1]
        psXg, psYe = [psX, psT0], [psY, psT1]

        ld_x = [sem("ld_x0"), sem("ld_x1")]
        ld_proj = sem("ld_proj")
        ld_small = sem("ld_small")
        ld_w1 = sem("ld_w1")
        ld_w2 = sem("ld_w2")
        bias_rows_in = sem("bias_rows_in")
        consts = sem("consts")
        pool_step = sem("pool_step")
        dve_step = sem("dve_step")
        act_step = sem("act_step")
        bias_split = sem("bias_split")
        dec_ready = sem("dec_ready")
        omt_ready = sem("omt_ready")
        wT_ps = sem("wT_ps")
        wT_ready = sem("wT_ready")
        var_ready = sem("var_ready")
        std_ready = sem("std_ready")
        ln_ready = sem("ln_ready")
        xn_pool = sem("xn_pool")
        xn_dve = sem("xn_dve")
        xn_stored = sem("xn_stored")
        xnT_ps = sem("xnT_ps")
        xnT_ready = sem("xnT_ready")
        mixed_a = sem("mixed_a")
        xm_ready = sem("xm_ready")
        gates = sem("gates")
        oh_ready = sem("oh_ready")
        prefix_ready = sem("prefix_ready")
        onehots = sem("onehots")
        inv_ps = sem("inv_ps")
        idx_ready = sem("idx_ready")
        experts_ready = sem("experts_ready")
        kvr_ps = [sem("k_ps"), sem("v_ps"), sem("r_ps")]
        kvr_out = [sem("k_out"), sem("v_out"), sem("r_out")]
        gidx_staged = sem("gidx_staged")
        sidx_staged = sem("sidx_staged")
        gathered = [sem(f"gathered{j}") for j in range(RING)]
        scattered = [sem(f"scattered{j}") for j in range(RING)]
        xgT_ps = sem("xgT_ps")
        layer1_in = sem("layer1_in")
        hid_ps = sem("hid_ps")
        hid_ready = sem("hid_ready")
        sel_ready = sem("sel_ready")
        y_ps = sem("y_ps")
        sgm_ready = sem("sgm_ready")
        g_ready = sem("g_ready")
        sig_ready = sem("sig_ready")
        k_capped = sem("k_capped")
        k_ready = sem("k_ready")
        den_ready = sem("den_ready")
        den_eps = sem("den_eps")
        rw_ready = sem("rw_ready")
        s_ps = sem("s_ps")
        s_ready = sem("s_ready")
        g_loaded = [sem("g_loaded0"), sem("g_loaded1")]
        prod_ready = sem("prod_ready")
        out_pool = sem("out_pool")
        out_dve = sem("out_dve")
        stored = sem("stored")
        NCONST = 15

        x_v = x.rearrange("b (n p) d -> p (b n) d", p=P)
        out_v = out.rearrange("b (n p) d -> p (b n) d", p=P)
        xn_v = xn_rows.rearrange("(n p) d -> p n d", p=P)
        g_v = g_rows[0:TOK, :].rearrange("(n p) d -> p n d", p=P)
        HALF = NT // 2
        block = ctx.enter_context(nc.Block())

        @block.sync
        def _(sp):
            for b in range(BATCH):
                sp.dma_start(x_sb[:, b * HALF:(b + 1) * HALF, :],
                             x_v[:, b * HALF:(b + 1) * HALF, :]).then_inc(ld_x[b], 16)
            sp.wait_ge(ld_small, 16 * 7)
            sp.wait_ge(ld_proj, 16 * 4)
            sp.dma_start(w1[:, :, :], W1.rearrange("e d h -> d e h")).then_inc(ld_w1, 16)
            sp.dma_start(w2[:, :, :], W2.rearrange("e (c p) d -> p (e c) d", p=P)).then_inc(ld_w2, 16)
            sp.wait_ge(bias_split, 1)
            n1 = E * HID // P
            for j in range(3):
                rows = bias_mat[j * E:(j + 1) * E, :]
                sp.dma_start(rows[:, 0:HID].rearrange("e (p c) -> e p c", c=n1),
                             bias_part[:, j, 0:n1]).then_inc(bias_rows_in, 16)
                sp.dma_start(rows[:, HID:].rearrange("e (p c) -> e p c", c=E),
                             bias_part[:, j, n1:]).then_inc(bias_rows_in, 16)
            for b in range(BATCH):
                sp.wait_ge(xn_pool, NBB * (b + 1))
                sp.wait_ge(xn_dve, NBB * (b + 1))
                sp.dma_start(xn_v[:, b * HALF:(b + 1) * HALF, :],
                             xn_sb[:, b * HALF:(b + 1) * HALF, :]).then_inc(xn_stored, 16)
            for j in range(RING):
                sp.wait_ge(scattered[j], 16 * TURNS)
            sp.wait_ge(rw_ready, NB)
            for b in range(BATCH):
                sp.dma_start(g_sb[:, b * HALF:(b + 1) * HALF, :],
                             g_v[:, b * HALF:(b + 1) * HALF, :]).then_inc(g_loaded[b], 16)
            for c in range(NB):
                if c % 2:
                    sp.wait_ge(out_pool, c // 2 + 1)
                else:
                    sp.wait_ge(out_dve, c // 2 + 1)
                sp.dma_start(out_v[:, c * TPB:(c + 1) * TPB, :],
                             g_sb[:, c * TPB:(c + 1) * TPB, :]).then_inc(stored, 16)
            sp.wait_ge(stored, 16 * NB)

        @block.gpsimd
        def _(pool):
            g = nc.gpsimd
            step = Steps(pool, pool_step)
            step.link(g.memset(ident[:, :], 0.0))
            g.affine_select(out=ident[:, :], in_=ident[:, :], compare_op=ALU.not_equal, fill=1.0, base=0,
                            pattern=[[-1, P]], channel_multiplier=1).then_inc(consts, 1)
            step.link(g.memset(upper[:, :], 1.0))
            g.affine_select(out=upper[:, :], in_=upper[:, :], compare_op=ALU.is_gt, fill=0.0, base=0,
                            pattern=[[1, P]], channel_multiplier=-1).then_inc(consts, 1)
            g.memset(ones[:, :], 1.0).then_inc(consts, 1)
            step.link(g.memset(keep[:, :], 1.0))
            g.memset(keep[:, :].rearrange("p (b k) -> p b k", b=BATCH)[:, :, 0], 0.0).then_inc(consts, 1)
            step.link(g.memset(going[:, :, :], 1.0))
            g.memset(going[:, :, 0], 0.0).then_inc(consts, 1)
            g.memset(one8[:, :], 1.0).then_inc(consts, 1)
            g.memset(xnT[:, :, 0], 0.0).then_inc(consts, 1)
            for n in range(1, TAYLOR + 1):
                last = g.memset(minus_over_n[:, n - 1:n], -1.0 / n)
            last.then_inc(consts, 1)
            g.iota(first[:, :], pattern=[[-1, E]], base=E, channel_multiplier=0,
                   allow_small_or_imprecise_dtypes=True).then_inc(consts, 1)
            g.iota(iota_h[:, :], pattern=[[1, P]], base=0, channel_multiplier=0,
                   allow_small_or_imprecise_dtypes=True).then_inc(consts, 1)
            g.iota(iota_s[:, :], pattern=[[1, NS]], base=0, channel_multiplier=0,
                   allow_small_or_imprecise_dtypes=True).then_inc(consts, 1)
            g.iota(tokc[:, :], pattern=[[P, NT]], base=-TOK // 2, channel_multiplier=1,
                   allow_small_or_imprecise_dtypes=True).then_inc(consts, 1)
            g.iota(padrow[:, :], pattern=[[P, NS]], base=TOK, channel_multiplier=1,
                   allow_small_or_imprecise_dtypes=True).then_inc(consts, 1)
            g.iota(row_i[:, 0:1], pattern=[[0, 1]], base=0, channel_multiplier=1).then_inc(consts, 1)
            g.memset(zk[:, :], 0.0)
            g.memset(zkv[:, :], 0.0).then_inc(consts, 1)

            pool.wait_ge(ln_ready, 1)
            for k in range(NB):
                for j in range(2):
                    n = k * TPB + j
                    last = g.tensor_scalar(xn_sb[:, n, :], x_sb[:, n, :], rstd[:, n:n + 1], nbias[:, n:n + 1],
                                           ALU.mult, ALU.add)
                last.then_inc(xn_pool, 1)
            def counted(count):
                return count if isinstance(count, int) else pool.compute_val(count)

            def stage_gather(i, j):
                pool.wait_ge(xgT_ps, i * RING + (j + 2))
                g.tensor_copy(gi[:, j:j + 2], gidx[:, bass.ds((i + 1) * RING + j, 2)]).then_inc(gidx_staged, 1)

            def gather(i, j):
                staged = counted(i * 2 + (j // 2 + 1))
                pool.wait_ge(xn_stored, 16 * BATCH)
                pool.wait_ge(gidx_staged, staged)
                g.indirect_dma_start(xg[j][:, :], None, xn_rows,
                                     bass.IndirectOffsetOnAxis(gi[:, j:j + 1], 0)).then_inc(gathered[j], 16)

            def stage_scatter(i, j):
                if not isinstance(i, int) or i:
                    pool.wait_ge(scattered[j], i * 16)
                    pool.wait_ge(scattered[j + 1], i * 16)
                g.tensor_copy(si[:, j:j + 2], sidx[:, bass.ds(i * RING + j, 2)]).then_inc(sidx_staged, 1)

            def scatter(i, j):
                gated = counted(i * RING + (j + 1))
                staged = counted(i * 2 + (j // 2 + 1))
                pool.wait_ge(idx_ready, 1)
                pool.wait_ge(g_ready, gated)
                pool.wait_ge(sidx_staged, staged)
                g.indirect_dma_start(g_rows, bass.IndirectOffsetOnAxis(si[:, j:j + 1], 0), gout[j][:, :],
                                     None).then_inc(scattered[j], 16)

            pool.wait_ge(idx_ready, 1)
            pool.wait_ge(xn_stored, 16 * BATCH)
            g.tensor_copy(gi[:, :], gidx[:, 0:RING]).then_inc(pool_step, 1)
            pool.wait_ge(pool_step, step.n + 1)
            for j in range(RING):
                g.indirect_dma_start(xg[j][:, :], None, xn_rows,
                                     bass.IndirectOffsetOnAxis(gi[:, j:j + 1], 0)).then_inc(gathered[j], 16)

            def turn(i, first=False, last=False):
                for j in range(RING):
                    if j % 2 == 0:
                        if not last:
                            stage_gather(i, j)
                        if j == 2:
                            stage_scatter(i, 0)
                        elif not first:
                            stage_scatter(i - 1, 2)
                    if not last:
                        gather(i, j)
                    if j >= 2:
                        scatter(i, j - 2)
                    elif not first:
                        scatter(i - 1, j + 2)

            turn(0, first=True)
            turn(1)
            with pool.Fori(2, TURNS - 1) as i:
                turn(i)
            turn(TURNS - 1, last=True)
            stage_scatter(TURNS - 1, 2)
            for j in range(2, RING):
                scatter(TURNS - 1, j)
            for c in range(1, NB, 2):
                pool.wait_ge(prod_ready, c + 1)
                g.tensor_tensor(g_sb[:, c * TPB:(c + 1) * TPB, :], g_sb[:, c * TPB:(c + 1) * TPB, :],
                                x_sb[:, c * TPB:(c + 1) * TPB, :], ALU.add).then_inc(out_pool, 1)

        @block.vector
        def _(dve):
            v = nc.vector
            step = Steps(dve, dve_step)
            for b in range(BATCH):
                dve.wait_ge(ld_x[b], 16)
                for n in range(b * HALF, (b + 1) * HALF):
                    last = v.bn_stats(stats[:, n, :], x_sb[:, n, :])
            step.link(last)
            dve.wait_ge(ld_small, 16 * 7)
            dve.wait_ge(consts, NCONST)
            v.tensor_scalar(omt[:, :], tmix[:, :], -1.0, 1.0, ALU.mult, ALU.add).then_inc(omt_ready, 1)
            step.link(v.tensor_copy(bias_part[:, 0, :], bias_nat[:, :]))
            step.link(v.tensor_tensor(bias_r[:, 0, :], bias_nat[:, :], bias_part[:, 0, :], ALU.subtract))
            step.link(v.tensor_copy(bias_part[:, 1, :], bias_r[:, 0, :]))
            step.link(v.tensor_tensor(bias_r[:, 1, :], bias_r[:, 0, :], bias_part[:, 1, :], ALU.subtract))
            v.tensor_copy(bias_part[:, 2, :], bias_r[:, 1, :]).then_inc(bias_split, 1)
            dve.wait_ge(dec_ready, 1)
            step.link(v.tensor_scalar(ydec[:, :], dec[:, :], SMALL_DECAY, None, ALU.min))
            v.tensor_scalar(small[:, :], dec[:, :], SMALL_DECAY, None, ALU.is_le)
            step.link(v.tensor_scalar(ytab[:, :], minus_over_n[:, :], ydec[:, 0:1], None, ALU.mult))
            v.tensor_scalar(large[:, :], small[:, :], -1.0, 1.0, ALU.mult, ALU.add)
            step.link(v.tensor_scalar(ser[:, :], ytab[:, TAYLOR - 1:TAYLOR], 1.0, None, ALU.add))
            for n in range(TAYLOR - 1, 0, -1):
                step.link(v.tensor_scalar(ser[:, :], ser[:, :], ytab[:, n - 1:n], 1.0, ALU.mult, ALU.add))
            step.link(v.tensor_tensor(ser[:, :], ser[:, :], small[:, :], ALU.mult))
            step.link(v.scalar_tensor_tensor(out=a[:, :], in0=a_exp[:, :], scalar=large[:, 0:1],
                                             in1=ser[:, :], op0=ALU.mult, op1=ALU.add))

            v.tensor_tensor(msum[:, :], stats[:, :, 1], stats[:, :, 4], ALU.add)
            step.link(v.tensor_tensor(mdif[:, :], stats[:, :, 1], stats[:, :, 4], ALU.subtract))
            v.tensor_tensor(var[:, :], stats[:, :, 2], stats[:, :, 5], ALU.add)
            step.link(v.scalar_tensor_tensor(out=newt[:, :], in0=mdif[:, :], scalar=0.25, in1=mdif[:, :],
                                             op0=ALU.mult, op1=ALU.mult))
            step.link(v.scalar_tensor_tensor(out=var[:, :], in0=var[:, :], scalar=1.0 / P, in1=newt[:, :],
                                             op0=ALU.mult, op1=ALU.add))
            ins = v.tensor_scalar(var[:, :], var[:, :], LN_EPS, None, ALU.add)
            ins.then_inc(var_ready, 1)
            dve.wait_ge(var_ready, 1)
            dve.wait_ge(std_ready, 1)
            step.link(v.reciprocal(rstd[:, :], std[:, :]))
            step.link(v.tensor_tensor(newt[:, :], rstd[:, :], rstd[:, :], ALU.mult))
            step.link(v.tensor_tensor(newt[:, :], newt[:, :], var[:, :], ALU.mult))
            step.link(v.tensor_scalar(newt[:, :], newt[:, :], -0.5, 1.5, ALU.mult, ALU.add))
            step.link(v.tensor_tensor(rstd[:, :], rstd[:, :], newt[:, :], ALU.mult))
            ins = v.scalar_tensor_tensor(out=nbias[:, :], in0=msum[:, :], scalar=-0.5, in1=rstd[:, :],
                                         op0=ALU.mult, op1=ALU.mult)
            ins.then_inc(ln_ready, 1)
            dve.wait_ge(ln_ready, 1)

            def mix_shifted(k):
                dve.wait_ge(mixed_a, k + 1)
                b, c = divmod(k, NBB)
                if c:
                    dve.wait_ge(xnT_ready, k + 1)
                v.scalar_tensor_tensor(out=xmT[:, k * BLK:(k + 1) * BLK], in0=xnT[:, b, c * BLK:(c + 1) * BLK],
                                       scalar=omt[:, 0:1], in1=xmT[:, k * BLK:(k + 1) * BLK],
                                       op0=ALU.mult, op1=ALU.add).then_inc(xm_ready, 1)

            for k in range(NB):
                for j in range(2, TPB):
                    n = k * TPB + j
                    last = v.tensor_scalar(xn_sb[:, n, :], x_sb[:, n, :], rstd[:, n:n + 1], nbias[:, n:n + 1],
                                           ALU.mult, ALU.add)
                last.then_inc(xn_dve, 1)
                if k >= 2:
                    if k == 2:
                        dve.wait_ge(omt_ready, 1)
                    mix_shifted(k - 2)
            mix_shifted(NB - 2)
            mix_shifted(NB - 1)

            dve.wait_ge(gates, NB)
            gate_ps = psG[:, 0:NT * E].rearrange("p (n e) -> p n e", e=E)
            step.link(v.tensor_tensor(logit[:, :, :], gate_ps, bgb[:, :].unsqueeze(1).to_broadcast([P, NT, E]),
                                      ALU.add))
            step.link(v.tensor_reduce(lmax[:, :], logit[:, :, :], AX.X, ALU.max))
            step.link(v.tensor_tensor(wsel[:, :, :], logit[:, :, :],
                                      lmax[:, :].unsqueeze(2).to_broadcast([P, NT, E]), ALU.is_equal))
            step.link(v.tensor_tensor(wsel[:, :, :], wsel[:, :, :],
                                      first[:, :].unsqueeze(1).to_broadcast([P, NT, E]), ALU.mult))
            step.link(v.tensor_reduce(wmax[:, :], wsel[:, :, :], AX.X, ALU.max))
            ins = v.tensor_tensor(oh[:, :, :].rearrange("p e n -> p n e"), wsel[:, :, :],
                                  wmax[:, :].unsqueeze(2).to_broadcast([P, NT, E]), ALU.is_equal)
            ins.then_inc(oh_ready, 1)
            dve.wait_ge(oh_ready, 1)
            dve.wait_ge(prefix_ready, 1)
            EN = E * NT
            flat = lambda t: t[:, :, :].rearrange("p e n -> p (e n)")
            step.link(v.tensor_copy(flat(tot), psS[:, EN:2 * EN]))
            step.link(v.tensor_tensor_scan(flat(incl), flat(going), flat(tot), 0.0, ALU.mult, ALU.add))
            v.tensor_tensor(flat(excl), flat(incl), flat(tot), ALU.subtract)
            step.link(v.tensor_scalar(cnt_i[:, 0, :], incl[:, :, NT - 1], float(P - 1), None, ALU.add))
            step.link(v.tensor_scalar(cnt_i[:, 1, :], cnt_i[:, 0, :], 7, None, ALU.logical_shift_right))
            step.link(v.tensor_copy(tiles_f[:, :], cnt_i[:, 1, :]))
            step.link(v.tensor_tensor_scan(end_t[:, :], one8[:, :], tiles_f[:, :], 0.0, ALU.mult, ALU.add))
            step.link(v.tensor_tensor(base_s[:, :], end_t[:, :], tiles_f[:, :], ALU.subtract))
            step.link(v.tensor_scalar(base_s[:, :], base_s[:, :], float(P), None, ALU.mult))
            step.link(v.tensor_tensor(flat(posw), psS[:, 0:EN], flat(excl), ALU.add))
            step.link(v.tensor_tensor(posw[:, :, :], posw[:, :, :],
                                      base_s[:, :].unsqueeze(2).to_broadcast([P, E, NT]), ALU.add))
            step.link(v.tensor_tensor(posw[:, :, :], posw[:, :, :], oh[:, :, :], ALU.mult))
            step.link(v.tensor_reduce(pos[:, :], posw[:, :, :].rearrange("p e n -> p n e"), AX.X, ALU.add))
            step.link(v.tensor_copy(pos_i[:, 0, :], pos[:, :]))
            v.tensor_scalar(pos_i[:, 1, :], pos_i[:, 0, :], 7, None, ALU.logical_shift_right)
            step.link(v.tensor_scalar(pos_i[:, 2, :], pos_i[:, 0, :], P - 1, None, ALU.bitwise_and))
            v.tensor_copy(hi_f[:, :], pos_i[:, 1, :])
            step.link(v.tensor_copy(lo_f[:, :], pos_i[:, 2, :]))
            step.link(v.tensor_tensor(ohhi[:, 1, :, :], iota_s[:, :].unsqueeze(1).to_broadcast([P, NT, NS]),
                                      hi_f[:, :].unsqueeze(2).to_broadcast([P, NT, NS]), ALU.is_equal))
            v.tensor_tensor(ohhi[:, 0, :, :], ohhi[:, 1, :, :],
                            tokc[:, :].unsqueeze(2).to_broadcast([P, NT, NS]), ALU.mult)
            for n in range(NT):
                last = v.tensor_scalar(ohlo[:, n, :], iota_h[:, :], lo_f[:, n:n + 1], None, ALU.is_equal)
            last.then_inc(onehots, 1)
            step.link(v.tensor_tensor(ecmp[:, :, :], iota_s[:, :].unsqueeze(2).to_broadcast([P, NS, E]),
                                      end_t[:, :].unsqueeze(1).to_broadcast([P, NS, E]), ALU.is_ge))
            step.link(v.tensor_reduce(esum[:, :], ecmp[:, :, :], AX.X, ALU.add))
            step.link(v.tensor_scalar(row_i[:, 1:2], row_i[:, 0:1], E - 1, None, ALU.bitwise_and))
            step.link(v.tensor_copy(row_e[:, :], row_i[:, 1:2]))
            v.tensor_scalar(sel[:, :], esum[0:BR, :], float(E - 1), row_e[:, 0:1], ALU.min, ALU.is_equal)
            v.tensor_scalar(etab[:, :], esum[:, :], float(E - 1), None, ALU.min).then_inc(experts_ready, 1)

            def cap_keys(b):
                dve.wait_ge(kvr_out[0], NBB * (b + 1))
                v.tensor_scalar(kT[:, b * T:(b + 1) * T], kT[:, b * T:(b + 1) * T], K_CLAMP, None,
                                ALU.min).then_inc(k_capped, 1)

            cap_keys(0)
            dve.wait_ge(inv_ps, 1)
            step.link(v.tensor_copy(inv[:, :, :].rearrange("p a s -> p (a s)"), psG[:, 0:2 * NS]))
            step.link(v.scalar_tensor_tensor(out=gidx_f[:, :], in0=inv[:, 1, :], scalar=float(TOK // 2),
                                             in1=inv[:, 0, :], op0=ALU.mult, op1=ALU.add))
            v.tensor_copy(gidx[:, :], gidx_f[:, :])
            step.link(v.tensor_tensor(pad_f[:, 0, :], inv[:, 1, :], padrow[:, :], ALU.mult))
            step.link(v.tensor_tensor(pad_f[:, 1, :], padrow[:, :], pad_f[:, 0, :], ALU.subtract))
            v.tensor_tensor(sidx[:, :], pad_f[:, 1, :], gidx_f[:, :], ALU.add).then_inc(idx_ready, 1)
            cap_keys(1)

            def gate_rows(i, j, reused):
                dve.wait_ge(sgm_ready, i * RING + (j + 1))
                if reused:
                    dve.wait_ge(scattered[j], i * 16)
                v.tensor_tensor(gout[j][:, :], psYe[j % 2][:, 0:P], sgm[j % 2][:, :],
                                ALU.mult).then_inc(g_ready, 1)

            def select_expert(i, j):
                return v.tensor_copy(sel_t[j][:, :], sel[:, bass.ds(i * RING + j, 1)].to_broadcast([BR, P]))

            def attend(i, part_no):
                q = i - 1
                here = bass.ds(q * BLK, BLK)
                step.n = step0 + q * LOOP_STEPS + done[0]
                if part_no == 0:
                    v.tensor_scalar(zkv[:, 0:1], zkv[:, BLK:BLK + 1], keep[:, bass.ds(q, 1)], None, ALU.mult)
                    v.tensor_scalar(zk[:, 0:1], zk[:, BLK:BLK + 1], keep[:, bass.ds(q, 1)], None, ALU.mult)
                    step.link(v.tensor_tensor(vT[:, here], kT[:, here], vT[:, here], ALU.mult))
                    step.link(v.tensor_tensor_scan(zk[:, 1:BLK + 1], a[:, 0:1].to_broadcast([P, BLK]),
                                                   kT[:, here], zk[:, 0:1], ALU.mult, ALU.add))
                    v.scalar_tensor_tensor(out=den[:, :], in0=kT[:, here], scalar=ef[:, 0:1],
                                           in1=zk[:, 0:BLK], op0=ALU.mult, op1=ALU.add).then_inc(den_ready, 1)
                    done[0] += 2
                elif part_no == 1:
                    step.link(v.tensor_tensor_scan(zkv[:, 1:BLK + 1], a[:, 0:1].to_broadcast([P, BLK]),
                                                   vT[:, here], zkv[:, 0:1], ALU.mult, ALU.add))
                    step.link(v.scalar_tensor_tensor(out=num[:, :], in0=vT[:, here], scalar=ef[:, 0:1],
                                                     in1=zkv[:, 0:BLK], op0=ALU.mult, op1=ALU.add))
                    dve.wait_ge(sig_ready, i)
                    v.tensor_tensor(signum[:, :], num[:, :], rT[:, here], ALU.mult)
                    done[0] += 2
                else:
                    half = slice((part_no - 2) * BLK // 2, (part_no - 1) * BLK // 2)
                    if part_no == 2:
                        dve.wait_ge(den_eps, i)
                    step.link(v.reciprocal(rden[:, half], den[:, half]))
                    if part_no == 2 and not isinstance(i, int):
                        dve.wait_ge(s_ps, i - 1)
                    last = v.tensor_tensor(rw[:, half], signum[:, half], rden[:, half], ALU.mult)
                    if part_no == 3:
                        last.then_inc(rw_ready, 1)
                    done[0] += 1

            LOOP_STEPS = 6
            done = [0]
            step0 = step.n

            def turn(i, first=False, last=False, attends=False):
                done[0] = 0
                for j in range(RING):
                    if attends:
                        attend(i, j)
                    if j < RING - 2:
                        if not first or j:
                            select_expert(i, j + 2)
                    elif not last:
                        select_expert(i + 1, j - 2)
                    if j:
                        gate_rows(i, j - 1, reused=not first)
                    elif not first:
                        gate_rows(i - 1, RING - 1, reused=not isinstance(i, int) or i > 1)

            select_expert(0, 0)
            select_expert(0, 1)
            select_expert(0, 2).then_inc(sel_ready, 1)
            turn(0, first=True)
            dve.wait_ge(k_ready, BATCH)
            dve.wait_ge(kvr_out[1], NB)
            turn(1, attends=True)
            with dve.Fori(2, TURNS - 1) as i:
                turn(i, attends=True)
            turn(TURNS - 1, last=True)
            gate_rows(TURNS - 1, RING - 1, reused=True)

            dve.wait_ge(s_ready, NB)
            for c in range(NB):
                if c % NBB == 0:
                    dve.wait_ge(g_loaded[c // NBB], 16)
                cols = slice(c * TPB, (c + 1) * TPB)
                v.tensor_tensor(g_sb[:, cols, :], g_sb[:, cols, :], s_sb[:, cols, :],
                                ALU.mult).then_inc(prod_ready, 1)
                if c % 2 == 0:
                    dve.wait_ge(prod_ready, c + 1)
                    v.tensor_tensor(g_sb[:, cols, :], g_sb[:, cols, :], x_sb[:, cols, :],
                                    ALU.add).then_inc(out_dve, 1)

        @block.scalar
        def _(act):
            s = nc.scalar
            act.dma_start(tmix[:, :], time_mix.rearrange("a b d -> d (a b)")).then_inc(ld_small, 16)
            act.dma_start(bgb[:, :], bg.rearrange("(o e) -> o e", o=1).to_broadcast([P, E])).then_inc(ld_small, 16)
            act.dma_start(wg[:, :], Wg).then_inc(ld_small, 16)
            act.dma_start(bias_nat[:, 0:E * HID // P],
                          b1.rearrange("e h -> (e h)").rearrange("(p c) -> p c", p=P)).then_inc(ld_small, 16)
            act.dma_start(bias_nat[:, E * HID // P:],
                          b2.rearrange("e h -> (e h)").rearrange("(p c) -> p c", p=P)).then_inc(ld_small, 16)
            act.dma_start(tdec[:, :], time_decay.to_broadcast([HEADS, HEAD])).then_inc(ld_small, 16)
            act.dma_start(tfir[:, :], time_first.to_broadcast([HEADS, HEAD])).then_inc(ld_small, 16)
            for t, w in enumerate((Wk, Wv, Wr, Wo)):
                act.dma_start(wnat[:, t, :], w).then_inc(ld_proj, 16)
            act.wait_ge(ld_small, 16 * 7)
            s.activation(dec[:, :], tdec[:, :], ACT.Exp).then_inc(act_step, 1)
            s.activation(ef[:, :], tfir[:, :], ACT.Exp)
            act.wait_ge(act_step, 1)
            s.activation(a_exp[:, :], dec[:, :], ACT.Exp, scale=-1.0).then_inc(dec_ready, 1)
            act.wait_ge(wT_ps, 1)
            s.copy(wT[:, :, :].rearrange("p t d -> p (t d)"), psX[:, :]).then_inc(wT_ready, 1)
            act.wait_ge(var_ready, 1)
            s.activation(std[:, :], var[:, :], ACT.Sqrt).then_inc(std_ready, 1)
            for k in range(NB):
                b, c = divmod(k, NBB)
                act.wait_ge(xnT_ps, k + 1)
                s.copy(xnT[:, b, 1 + c * BLK:1 + (c + 1) * BLK], psT[k % 2][:, :]).then_inc(xnT_ready, 1)
                s.mul(xmT[:, k * BLK:(k + 1) * BLK], psT[k % 2][:, :], tmix[:, 0:1]).then_inc(mixed_a, 1)

            def kvr(k):
                here = bass.ds(k * BLK, BLK)
                for t, (dst, ps) in enumerate(((kT, psH0), (vT, psH1), (rT, psY))):
                    act.wait_ge(kvr_ps[t], k + 1)
                    s.copy(dst[:, here], ps[:, :]).then_inc(kvr_out[t], 1)

            with act.Fori(0, NB) as k:
                kvr(k)

            def exp_k(b):
                act.wait_ge(k_capped, b + 1)
                s.activation(kT[:, b * T:(b + 1) * T], kT[:, b * T:(b + 1) * T], ACT.Exp).then_inc(k_ready, 1)

            def expert(i, j):
                return act.value_load(etab[0:1, bass.ds(i * RING + j, 1)], min_val=0, max_val=E - 1)

            def copy_w1(i, j):
                e = expert(i, j)
                s.copy(w1e[j % 2][:, :], w1[:, bass.ds(e, 1), :].rearrange("p o h -> p (o h)"))

            def copy_xgT(i, j):
                act.wait_ge(xgT_ps, i * RING + (j + 1))
                s.copy(xgT[j % 2][:, :], psXg[j % 2][:, 0:P]).then_inc(layer1_in, 1)

            def copy_w2(i, j):
                e = expert(i, j)
                s.copy(w2e[j % 2][:, :], w2[:, bass.ds(e * HC, HC), :].rearrange("p c d -> p (c d)"))

            def relu(i, j):
                act.wait_ge(hid_ps, i * RING + (j + 1))
                s.activation(hidT[j % 2][:, :], psH[j % 2][:, :], ACT.Relu).then_inc(hid_ready, 1)

            def sigmoid_y(i, j):
                act.wait_ge(y_ps, i * RING + (j + 1))
                if not isinstance(i, int) or i * RING + j >= 2:
                    act.wait_ge(g_ready, i * RING + (j - 1))
                s.activation(sgm[j % 2][:, :], psYe[j % 2][:, 0:P], ACT.Sigmoid).then_inc(sgm_ready, 1)

            def copy_s(i):
                act.wait_ge(s_ps, i - 1)
                s.copy(s_sb[:, bass.ds((i - 2) * TPB, TPB), :], psS[:, :].rearrange("p (n d) -> p n d", d=P)
                       ).then_inc(s_ready, 1)

            def turn(i, first=False, last=False, attends=False, projects=False):
                for j in range(RING):
                    if j < RING - 1:
                        copy_xgT(i, j + 1)
                    elif not last:
                        copy_xgT(i + 1, 0)
                    relu(i, j)
                    if j < RING - 2:
                        copy_w1(i, j + 2)
                    elif not last:
                        copy_w1(i + 1, j - 2)
                    if attends and j == 0:
                        here = bass.ds((i - 1) * BLK, BLK)
                        s.activation(rT[:, here], rT[:, here], ACT.Sigmoid).then_inc(sig_ready, 1)
                    if attends and j == 1:
                        act.wait_ge(den_ready, i)
                        s.activation(den[:, :], den[:, :], ACT.Copy, bias=K_EPS).then_inc(den_eps, 1)
                    if projects and j == 2:
                        copy_s(i)
                    if j:
                        sigmoid_y(i, j - 1)
                    elif not first:
                        sigmoid_y(i - 1, RING - 1)
                    if j < RING - 1:
                        copy_w2(i, j + 1)
                    elif not last:
                        copy_w2(i + 1, 0)

            act.wait_ge(experts_ready, 1)
            act.wait_ge(ld_w1, 16)
            exp_k(0)
            act.wait_ge(inv_ps, 1)
            copy_w1(0, 0)
            copy_xgT(0, 0)
            copy_w1(0, 1)
            act.wait_ge(ld_w2, 16)
            copy_w2(0, 0)
            exp_k(1)
            turn(0, first=True)
            act.wait_ge(kvr_out[2], NB)
            act.wait_ge(xn_stored, 16 * BATCH)
            turn(1, attends=True)
            with act.Fori(2, TURNS - 1) as i:
                turn(i, attends=True, projects=True)
            turn(TURNS - 1, last=True, projects=True)
            sigmoid_y(TURNS - 1, RING - 1)

        @block.tensor
        def _(pe):
            t = nc.tensor
            pe.wait_ge(consts, NCONST)
            pe.wait_ge(ld_proj, 16 * 4)
            for m in range(4):
                last = t.transpose(psX[:, m * P:(m + 1) * P], wnat[:, m, :], ident[:, :])
            last.then_inc(wT_ps, 1)

            def logits(k):
                b, c = divmod(k, NBB)
                pe.wait_ge(xnT_ready, k + 1)
                for j in range(TPB):
                    n = k * TPB + j
                    c0 = 1 + c * BLK + j * P
                    last = t.matmul(psG[:, n * E:(n + 1) * E], xnT[:, b, c0:c0 + P], wg[:, :],
                                    start=True, stop=True)
                last.then_inc(gates, 1)

            for k in range(NB):
                pe.wait_ge(xn_pool, k + 1)
                pe.wait_ge(xn_dve, k + 1)
                if k >= 2:
                    pe.wait_ge(mixed_a, k - 1)
                for j in range(TPB):
                    last = t.transpose(psT[k % 2][:, j * P:(j + 1) * P], xn_sb[:, k * TPB + j, :], ident[:, :])
                last.then_inc(xnT_ps, 1)
                if k == 1:
                    pe.wait_ge(ld_small, 16 * 7)
                if k:
                    logits(k - 1)
            logits(NB - 1)

            pe.wait_ge(wT_ready, 1)

            def kvr(k, first=False):
                pe.wait_ge(xm_ready, k + 1)
                for m, ps in enumerate((psH0, psH1, psY)):
                    if not first:
                        pe.wait_ge(kvr_out[m], k)
                    t.matmul(ps[:, :], wT[:, m, :], xmT[:, bass.ds(k * BLK, BLK)],
                             start=True, stop=True).then_inc(kvr_ps[m], 1)

            def prefix():
                pe.wait_ge(oh_ready, 1)
                EN = E * NT
                ohf = oh[:, :, :].rearrange("p e n -> p (e n)")
                t.matmul(psS[:, 0:EN], upper[:, :], ohf, start=True, stop=True)
                t.matmul(psS[:, EN:2 * EN], ones[:, :], ohf, start=True, stop=True).then_inc(prefix_ready, 1)

            kvr(0, first=True)
            prefix()
            with pe.Fori(1, NB - 2) as k:
                kvr(k)

            pe.wait_ge(onehots, 1)
            for n in range(NT):
                last = t.matmul(psG[:, 0:2 * NS].rearrange("p (a s) -> p a s", a=2), ohlo[:, n, :],
                                ohhi[:, :, n, :], start=(n == 0), stop=(n == NT - 1))
            last.then_inc(inv_ps, 1)
            for k in range(NB - 2, NB):
                kvr(k)

            def transpose_rows(i, j):
                pe.wait_ge(gathered[j], (i + 1) * 16)
                t.transpose(psXg[j % 2][:, 0:P], xg[j][:, :], ident[:, :]).then_inc(xgT_ps, 1)

            def layer1(i, j):
                if isinstance(i, int) and i * RING + j < 3:
                    pe.wait_ge(sel_ready, 1)
                else:
                    pe.wait_ge(g_ready, i * RING + (j - 2) if j >= 2 else (i - 1) * RING + (j + 2))
                pe.wait_ge(layer1_in, i * RING + (j + 1))
                for c in range(HC):
                    cols = slice(c * P, (c + 1) * P)
                    t.matmul(psH[j % 2][:, cols], bias_mat[:, cols], sel_t[j][:, :], start=True, stop=False)
                    last = t.matmul(psH[j % 2][:, cols], w1e[j % 2][:, cols], xgT[j % 2][:, :],
                                    start=False, stop=True)
                last.then_inc(hid_ps, 1)

            def layer2(i, j):
                pe.wait_ge(hid_ready, i * RING + (j + 1))
                for c in range(HC):
                    cols = slice(c * P, (c + 1) * P)
                    t.matmul(psYe[j % 2][:, 0:P], hidT[j % 2][:, cols], w2e[j % 2][:, cols],
                             start=(c == 0), stop=False)
                t.matmul(psYe[j % 2][:, 0:P], sel_t[j][:, :], bias_mat[:, HID:],
                         start=False, stop=True).then_inc(y_ps, 1)

            def project(i):
                pe.wait_ge(rw_ready, i - 1)
                if not isinstance(i, int) or i > 2:
                    pe.wait_ge(s_ready, i - 2)
                for j in range(TPB):
                    last = t.matmul(psS[:, j * P:(j + 1) * P], rw[:, j * P:(j + 1) * P], wT[:, 3, :],
                                    start=True, stop=True)
                last.then_inc(s_ps, 1)

            def turn(i, first=False, last=False, projects=False):
                for j in range(RING):
                    if j < RING - 1:
                        transpose_rows(i, j + 1)
                    elif not last:
                        transpose_rows(i + 1, 0)
                    layer1(i, j)
                    if j:
                        layer2(i, j - 1)
                    elif not first:
                        layer2(i - 1, RING - 1)
                    if projects and j == 1:
                        project(i)

            pe.wait_ge(bias_rows_in, 16 * 6)
            for m in range(3):
                pe.wait_ge(kvr_out[m], NB)
            transpose_rows(0, 0)
            turn(0, first=True)
            turn(1)
            turn(2, projects=True)
            with pe.Fori(3, TURNS - 1) as i:
                turn(i, projects=True)
            turn(TURNS - 1, last=True, projects=True)
            pe.wait_ge(g_ready, NS - 2)
            layer2(TURNS - 1, RING - 1)


_INS = ['L0_attn_x', 'L0_attn_time_decay', 'L0_attn_time_first', 'L0_attn_time_mix', 'L0_attn_Wk', 'L0_attn_Wv',
        'L0_attn_Wr', 'L0_attn_Wo', 'L0_ffn_Wg', 'L0_ffn_bg', 'L0_ffn_W1', 'L0_ffn_b1', 'L0_ffn_W2', 'L0_ffn_b2']


def kernel(**inputs):
    import numpy as _np
    import concourse.bacc as _bacc
    from concourse import mybir as _mybir
    from concourse.bass_utils import run_bass_kernel_spmd as _run

    nc = _bacc.Bacc("TRN2", target_bir_lowering=False, num_devices=1)
    arrays, args = {}, []
    for name in _INS:
        arr = _np.ascontiguousarray(inputs[name])
        arrays[f"in_{name}"] = arr
        args.append(nc.dram_tensor(f"in_{name}", arr.shape, _mybir.dt.from_np(arr.dtype), kind="ExternalInput").ap())
    args.append(nc.dram_tensor("out_x", (BATCH, T, P), F32, kind="ExternalOutput").ap())
    mixture_kernel(nc, *args)
    r = _run(nc, [arrays], core_ids=[0])
    return r.results[0]["out_x"]
```

```python
from contextlib import ExitStack

import concourse.bass as bass
from concourse import mybir

F32 = mybir.dt.float32
BF16 = mybir.dt.bfloat16
F16 = mybir.dt.float16
I32 = mybir.dt.int32
ALU = mybir.AluOpType
ACT = mybir.ActivationFunctionType
AX = mybir.AxisListType

P = 128
BATCH, T = 2, 2048
TOK = BATCH * T
NT = TOK // P
BLK = 512
TPB = BLK // P
NB = TOK // BLK
NBB = NB // BATCH
HEADS = 16
HEAD = P // HEADS
E = 8
HID = 512
HC = HID // P
RING = 4
SLOTS = NT + E - 1
TURNS = -(-SLOTS // RING)
LAST = SLOTS - (TURNS - 1) * RING
NS = TURNS * RING
SPARE = NS * P
XLOADS = 8
STAT = 6
LN_EPS = 1e-5
K_EPS = 1e-16
K_CLAMP = 60.0
WARM_UP = 36
ACT_BLOCKS = NB - 2
POOL_ADDS = (1, 3, 5)
POOL_TILES = 5
TAYLOR = 9
SMALL_DECAY = 0.5
BR = 3 * E


class Steps:

    def __init__(self, eng, sem):
        self.eng, self.sem, self.n = eng, sem, 0

    def link(self, ins, meanwhile=None):
        ins.then_inc(self.sem, 1)
        self.n = self.n + 1
        if meanwhile:
            meanwhile()
        self.eng.wait_ge(self.sem, self.n)


def mixture_kernel(nc, x, time_decay, time_first, time_mix, Wk, Wv, Wr, Wo, Wg, bg, W1, b1, W2, b2, out):
    ctx = ExitStack()
    with ctx:
        def sb(name, shape, dt=F32):
            return ctx.enter_context(nc.sbuf_tensor(name, shape, dt))

        def bank(name):
            return ctx.enter_context(nc.psum_tensor(name, [P, BLK], F32))

        def sem(name):
            return ctx.enter_context(nc.semaphore(name))

        xn_rows = nc.dram_tensor("xn_rows", [TOK, P], F32).ap()
        g_rows = nc.dram_tensor("g_rows", [TOK + SPARE, P], F32).ap()

        x_sb = sb("x_sb", [P, NT, P])
        xn_sb = sb("xn_sb", [P, NT, P])
        s_sb = xn_sb
        xnT = sb("xnT", [P, BATCH, T + 1])
        xmT = sb("xmT", [P, TOK])
        kT = sb("kT", [P, TOK])
        vT = sb("vT", [P, TOK])
        rT = sb("rT", [P, TOK])
        g_sb = kT[:, :].rearrange("p (n d) -> p n d", d=P)
        w1 = sb("w1", [P, E, HID])
        w2 = sb("w2", [P, E * HC, P])
        wnat = sb("wnat", [P, 4, P])
        wT = sb("wT", [P, 4, P])
        wg = sb("wg", [P, E])
        bgb = sb("bgb", [P, E])
        bias_nat = sb("bias_nat", [P, (E * HID + E * P) // P])
        bias_r = sb("bias_r", [P, 2, (E * HID + E * P) // P])
        bias_part = sb("bias_part", [P, 3, (E * HID + E * P) // P], BF16)
        bias_mat = sb("bias_mat", [BR, HID + P], BF16)
        tmix = sb("tmix", [P, 1])
        omt = sb("omt", [P, 1])
        tdec = sb("tdec", [P, 1])
        tfir = sb("tfir", [P, 1])
        dec = sb("dec", [P, 1])
        small = sb("small", [P, 1])
        large = sb("large", [P, 1])
        ydec = sb("ydec", [P, 1])
        minus_over_n = sb("minus_over_n", [P, TAYLOR])
        ytab = sb("ytab", [P, TAYLOR])
        ser = sb("ser", [P, 1])
        a_exp = sb("a_exp", [P, 1])
        a = sb("a", [P, 1])
        ef = sb("ef", [P, 1])
        ident = sb("ident", [P, P])
        upper = sb("upper", [P, P], BF16)
        ones = sb("ones", [P, P], BF16)
        keep = sb("keep", [P, NB])
        stats = sb("stats", [P, NT, STAT])
        msum = sb("msum", [P, NT])
        mdif = sb("mdif", [P, NT])
        var = sb("var", [P, NT])
        std = sb("std", [P, NT])
        rstd = sb("rstd", [P, NT])
        newt = sb("newt", [P, NT])
        nbias = sb("nbias", [P, NT])
        logit = sb("logit", [P, NT, E])
        lmax = sb("lmax", [P, NT])
        first = sb("first", [P, E])
        wsel = sb("wsel", [P, NT, E])
        wmax = sb("wmax", [P, NT])
        oh = sb("oh", [P, E, NT], BF16)
        going = sb("going", [P, E, NT])
        tot = sb("tot", [P, E, NT])
        incl = sb("incl", [P, E, NT])
        excl = sb("excl", [P, E, NT])
        cnt_i = sb("cnt_i", [P, 2, E], I32)
        tiles_f = sb("tiles_f", [P, E])
        one8 = sb("one8", [P, E])
        end_t = sb("end_t", [P, E])
        base_s = sb("base_s", [P, E])
        posw = sb("posw", [P, E, NT])
        pos = sb("pos", [P, NT])
        pos_i = sb("pos_i", [P, 3, NT], I32)
        hi_f = sb("hi_f", [P, NT])
        lo_f = sb("lo_f", [P, NT])
        iota_s = sb("iota_s", [P, NS])
        padrow = sb("padrow", [P, NS])
        iota_h = sb("iota_h", [P, P], F16)
        tokc = sb("tokc", [P, NT])
        ohlo = sb("ohlo", [P, NT, P], F16)
        ohhi_hidif = sb("ohhi_hidif", [P, 2, NT, NS], F16)
        ohhi, hidif = ohhi_hidif[:, 0, :, :], ohhi_hidif[:, 1, :, :]
        inv = sb("inv", [P, NS])
        upper_half = sb("upper_half", [P, NS])
        presence = sb("presence", [P, NS])
        gidx_f = sb("gidx_f", [P, NS])
        pad_f = sb("pad_f", [P, 2, NS])
        gidx = sb("gidx", [P, NS], I32)
        sidx = sb("sidx", [P, NS], I32)
        ecmp = sb("ecmp", [P, NS, E])
        esum = sb("esum", [P, NS])
        etab = sb("etab", [P, NS], I32)
        row_i = sb("row_i", [BR, 2], I32)
        row_e = sb("row_e", [BR, 1])
        sel = sb("sel", [BR, NS], BF16)
        gi = sb("gi", [P, RING], I32)
        si = sb("si", [P, RING], I32)
        xg = [sb(f"xg{j}", [P, P]) for j in range(RING)]
        xgT = [sb(f"xgT{j}", [P, P]) for j in range(2)]
        sel_t = [sb(f"sel_t{j}", [BR, P], BF16) for j in range(RING)]
        w1e = [sb(f"w1e{j}", [P, HID]) for j in range(2)]
        w2e = [sb(f"w2e{j}", [P, HID]) for j in range(2)]
        sgm = [sb(f"sgm{j}", [P, P]) for j in range(2)]
        gout = [sb(f"gout{j}", [P, P]) for j in range(RING)]
        z = sb("z", [P, 2, BLK + 1])
        zk, zkv = z[:, 0, :], z[:, 1, :]
        ohhi_f = ohhi_hidif[:, :, :, :].rearrange("p a n s -> p (a n s)").bitcast(F32)
        hidT = [ohhi_f[:, m * HID:(m + 1) * HID] for m in range(2)]
        rw = sb("rw", [P, BLK])
        ohlo_f = ohlo[:, :, :].rearrange("p n s -> p (n s)").bitcast(F32)
        den, rden, num, signum = (ohlo_f[:, m * BLK:(m + 1) * BLK] for m in range(4))

        psX, psH0, psH1, psT0, psT1, psY, psS, psG = [bank(f"ps{i}") for i in range(8)]
        psH, psT = [psH0, psH1], [psT0, psT1]
        psXg, psYe = [psX, psT0], [psY, psT1]

        ld_x = [sem(f"ld_x{j}") for j in range(XLOADS)]
        ld_proj = sem("ld_proj")
        ld_small = sem("ld_small")
        ld_w1 = sem("ld_w1")
        ld_w2 = sem("ld_w2")
        bias_rows_in = sem("bias_rows_in")
        ones_ready = sem("ones_ready")
        consts = sem("consts")
        pool_step = sem("pool_step")
        dve_step = sem("dve_step")
        act_step = sem("act_step")
        bias_split = sem("bias_split")
        dec_ready = sem("dec_ready")
        decay_ready = sem("decay_ready")
        omt_ready = sem("omt_ready")
        wT_ps = sem("wT_ps")
        wT_ready = sem("wT_ready")
        var_ready = sem("var_ready")
        std_ready = sem("std_ready")
        ln_ready = sem("ln_ready")
        xn_pool = sem("xn_pool")
        xn_dve = sem("xn_dve")
        xn_stored = sem("xn_stored")
        xnT_ps = sem("xnT_ps")
        xnT_ready = sem("xnT_ready")
        mixed_a = sem("mixed_a")
        xm_ready = sem("xm_ready")
        gates = sem("gates")
        oh_ready = sem("oh_ready")
        prefix_ready = sem("prefix_ready")
        slots_ready = sem("slots_ready")
        onehots = sem("onehots")
        onehots_pool = sem("onehots_pool")
        hidif_ready = sem("hidif_ready")
        inv_ps = sem("inv_ps")
        gidx_ready = sem("gidx_ready")
        idx_ready = sem("idx_ready")
        experts_ready = sem("experts_ready")
        kvr_ps = [sem("k_ps"), sem("v_ps"), sem("r_ps")]
        kvr_out = [sem("k_out"), sem("v_out"), sem("r_out")]
        gidx_staged = sem("gidx_staged")
        sidx_staged = sem("sidx_staged")
        gathered = [sem(f"gathered{j}") for j in range(RING)]
        scattered = [sem(f"scattered{j}") for j in range(RING)]
        xgT_ps = sem("xgT_ps")
        layer1_in = sem("layer1_in")
        hid_ps = sem("hid_ps")
        hid_ready = sem("hid_ready")
        sel_ready = sem("sel_ready")
        y_ps = sem("y_ps")
        sgm_ready = sem("sgm_ready")
        g_ready = sem("g_ready")
        sig_ready = sem("sig_ready")
        k_capped = sem("k_capped")
        k_ready = sem("k_ready")
        den_ready = sem("den_ready")
        den_eps = sem("den_eps")
        rw_ready = sem("rw_ready")
        s_ps = sem("s_ps")
        s_ready = sem("s_ready")
        g_loaded = [sem(f"g_loaded{c}") for c in range(NB)]
        prod_ready = sem("prod_ready")
        out_pool = sem("out_pool")
        out_dve = sem("out_dve")
        stored = sem("stored")
        NCONST_TOKC = 11
        NCONST = 15

        x_v = x.rearrange("b (n p) d -> p (b n) d", p=P)
        out_v = out.rearrange("b (n p) d -> p (b n) d", p=P)
        xn_v = xn_rows.rearrange("(n p) d -> p n d", p=P)
        g_v = g_rows[0:TOK, :].rearrange("(n p) d -> p n d", p=P)
        HALF = NT // 2
        block = ctx.enter_context(nc.Block())

        @block.sync
        def _(sp):
            for j in range(XLOADS):
                tiles = slice(j * NT // XLOADS, (j + 1) * NT // XLOADS)
                sp.dma_start(x_sb[:, tiles, :], x_v[:, tiles, :]).then_inc(ld_x[j], 16)
            for t, w in enumerate((Wk, Wv, Wr, Wo)):
                sp.dma_start(wnat[:, t, :], w).then_inc(ld_proj, 16)
            sp.dma_start(bias_nat[:, 0:E * HID // P],
                         b1.rearrange("e h -> (e h)").rearrange("(p c) -> p c", p=P)).then_inc(ld_small, 16)
            sp.dma_start(bias_nat[:, E * HID // P:],
                         b2.rearrange("e h -> (e h)").rearrange("(p c) -> p c", p=P)).then_inc(ld_small, 16)
            sp.wait_ge(ld_small, 16 * 7)
            sp.wait_ge(ld_proj, 16 * 4)
            sp.dma_start(w1[:, :, :], W1.rearrange("e d h -> d e h")).then_inc(ld_w1, 16)
            sp.dma_start(w2[:, :, :], W2.rearrange("e (c p) d -> p (e c) d", p=P)).then_inc(ld_w2, 16)
            sp.wait_ge(bias_split, 1)
            n1 = E * HID // P
            for j in range(3):
                rows = bias_mat[j * E:(j + 1) * E, :]
                sp.dma_start(rows[:, 0:HID].rearrange("e (p c) -> e p c", c=n1),
                             bias_part[:, j, 0:n1]).then_inc(bias_rows_in, 16)
                sp.dma_start(rows[:, HID:].rearrange("e (p c) -> e p c", c=E),
                             bias_part[:, j, n1:]).then_inc(bias_rows_in, 16)
            for b in range(BATCH):
                sp.wait_ge(xn_pool, NBB * (b + 1))
                sp.wait_ge(xn_dve, 2 * NBB * (b + 1))
                sp.dma_start(xn_v[:, b * HALF:(b + 1) * HALF, :],
                             xn_sb[:, b * HALF:(b + 1) * HALF, :]).then_inc(xn_stored, 16)
            for j in range(RING):
                sp.wait_ge(scattered[j], 16 * (TURNS if j < LAST else TURNS - 1))
            sp.wait_ge(rw_ready, NB)
            for c in range(NB):
                tiles = slice(c * TPB, (c + 1) * TPB)
                sp.dma_start(g_sb[:, tiles, :], g_v[:, tiles, :]).then_inc(g_loaded[c], 16)
            for c in range(NB):
                if c in POOL_ADDS:
                    sp.wait_ge(out_pool, POOL_ADDS.index(c) + 1)
                else:
                    sp.wait_ge(out_dve, c + 1 - sum(p < c for p in POOL_ADDS))
                sp.dma_start(out_v[:, c * TPB:(c + 1) * TPB, :],
                             g_sb[:, c * TPB:(c + 1) * TPB, :]).then_inc(stored, 16)
            sp.wait_ge(stored, 16 * NB)

        @block.gpsimd
        def _(pool):
            g = nc.gpsimd
            step = Steps(pool, pool_step)
            g.memset(ones[:, :], 1.0).then_inc(ones_ready, 1)
            step.link(g.memset(ident[:, :], 0.0))
            g.affine_select(out=ident[:, :], in_=ident[:, :], compare_op=ALU.not_equal, fill=1.0, base=0,
                            pattern=[[-1, P]], channel_multiplier=1).then_inc(consts, 1)
            step.link(g.memset(upper[:, :], 1.0))
            g.affine_select(out=upper[:, :], in_=upper[:, :], compare_op=ALU.is_gt, fill=0.0, base=0,
                            pattern=[[1, P]], channel_multiplier=-1).then_inc(consts, 1)
            step.link(g.memset(keep[:, :], 1.0))
            g.memset(keep[:, :].rearrange("p (b k) -> p b k", b=BATCH)[:, :, 0], 0.0).then_inc(consts, 1)
            step.link(g.memset(going[:, :, :], 1.0))
            g.memset(going[:, :, 0], 0.0).then_inc(consts, 1)
            g.memset(one8[:, :], 1.0).then_inc(consts, 1)
            g.memset(xnT[:, :, 0], 0.0).then_inc(consts, 1)
            for n in range(1, TAYLOR + 1):
                last = g.memset(minus_over_n[:, n - 1:n], -1.0 / n)
            last.then_inc(consts, 1)
            g.iota(first[:, :], pattern=[[-1, E]], base=E, channel_multiplier=0,
                   allow_small_or_imprecise_dtypes=True).then_inc(consts, 1)
            g.iota(iota_h[:, :], pattern=[[1, P]], base=0, channel_multiplier=0,
                   allow_small_or_imprecise_dtypes=True).then_inc(consts, 1)
            g.iota(iota_s[:, :], pattern=[[1, NS]], base=0, channel_multiplier=0,
                   allow_small_or_imprecise_dtypes=True).then_inc(consts, 1)
            g.iota(tokc[:, :], pattern=[[P, NT]], base=-TOK // 2, channel_multiplier=1,
                   allow_small_or_imprecise_dtypes=True).then_inc(consts, 1)
            pool.wait_ge(consts, NCONST_TOKC)
            g.tensor_scalar(tokc[:, NT // 2:], tokc[:, NT // 2:], 1.0, None, ALU.add).then_inc(consts, 1)
            g.iota(padrow[:, :], pattern=[[P, NS]], base=TOK, channel_multiplier=1,
                   allow_small_or_imprecise_dtypes=True).then_inc(consts, 1)
            g.iota(row_i[:, 0:1], pattern=[[0, 1]], base=0, channel_multiplier=1).then_inc(consts, 1)
            g.memset(z[:, :, :], 0.0).then_inc(consts, 1)

            for k in range(NB):
                if k % NBB == 0:
                    pool.wait_ge(ln_ready, k // NBB + 1)
                for j in range(2):
                    n = k * TPB + j
                    last = g.tensor_scalar(xn_sb[:, n, :], x_sb[:, n, :], rstd[:, n:n + 1], nbias[:, n:n + 1],
                                           ALU.mult, ALU.add)
                last.then_inc(xn_pool, 1)
            pool.wait_ge(ld_small, 16 * 7)
            step.link(g.tensor_copy(bias_part[:, 0, :], bias_nat[:, :]))
            step.link(g.tensor_tensor(bias_r[:, 0, :], bias_nat[:, :], bias_part[:, 0, :], ALU.subtract))
            step.link(g.tensor_copy(bias_part[:, 1, :], bias_r[:, 0, :]))
            step.link(g.tensor_tensor(bias_r[:, 1, :], bias_r[:, 0, :], bias_part[:, 1, :], ALU.subtract))
            g.tensor_copy(bias_part[:, 2, :], bias_r[:, 1, :]).then_inc(bias_split, 1)
            pool.wait_ge(dec_ready, 1)
            step.link(g.tensor_scalar(ydec[:, :], dec[:, :], SMALL_DECAY, None, ALU.min))
            g.tensor_scalar(small[:, :], dec[:, :], SMALL_DECAY, None, ALU.is_le)
            step.link(g.tensor_scalar(ytab[:, :], minus_over_n[:, :], ydec[:, 0:1], None, ALU.mult))
            g.tensor_scalar(large[:, :], small[:, :], -1.0, 1.0, ALU.mult, ALU.add)
            step.link(g.tensor_scalar(ser[:, :], ytab[:, TAYLOR - 1:TAYLOR], 1.0, None, ALU.add))
            for n in range(TAYLOR - 1, 0, -1):
                step.link(g.tensor_scalar(ser[:, :], ser[:, :], ytab[:, n - 1:n], 1.0, ALU.mult, ALU.add))
            g.tensor_tensor(ser[:, :], ser[:, :], small[:, :], ALU.mult)
            step.link(g.tensor_tensor(a_exp[:, :], a_exp[:, :], large[:, :], ALU.mult))
            g.tensor_tensor(a[:, :], a_exp[:, :], ser[:, :], ALU.add).then_inc(decay_ready, 1)

            pool.wait_ge(slots_ready, 1)
            g.tensor_tensor(hidif[:, :, :], iota_s[:, :].unsqueeze(1).to_broadcast([P, NT, NS]),
                            hi_f[:, :].unsqueeze(2).to_broadcast([P, NT, NS]), ALU.subtract
                            ).then_inc(hidif_ready, 1)
            for n in range(NT - POOL_TILES, NT):
                last = g.tensor_scalar(ohlo[:, n, :], iota_h[:, :], lo_f[:, n:n + 1], None, ALU.is_equal)
            last.then_inc(onehots_pool, 1)

            def counted(count):
                return count if isinstance(count, int) else pool.compute_val(count)

            def stage_gather(i, j):
                pool.wait_ge(xgT_ps, i * RING + (j + 2))
                g.tensor_copy(gi[:, j:j + 2], gidx[:, bass.ds((i + 1) * RING + j, 2)]).then_inc(gidx_staged, 1)

            def gather(i, j):
                staged = counted(i * 2 + (j // 2 + 1))
                pool.wait_ge(xn_stored, 16 * BATCH)
                pool.wait_ge(gidx_staged, staged)
                g.indirect_dma_start(xg[j][:, :], None, xn_rows,
                                     bass.IndirectOffsetOnAxis(gi[:, j:j + 1], 0)).then_inc(gathered[j], 16)

            def stage_scatter(i, j):
                if not isinstance(i, int) or i:
                    pool.wait_ge(scattered[j], i * 16)
                    pool.wait_ge(scattered[j + 1], i * 16)
                g.tensor_copy(si[:, j:j + 2], sidx[:, bass.ds(i * RING + j, 2)]).then_inc(sidx_staged, 1)

            def scatter(i, j):
                gated = counted(i * RING + (j + 1))
                staged = counted(i * 2 + (j // 2 + 1))
                pool.wait_ge(idx_ready, 1)
                pool.wait_ge(g_ready, gated)
                pool.wait_ge(sidx_staged, staged)
                g.indirect_dma_start(g_rows, bass.IndirectOffsetOnAxis(si[:, j:j + 1], 0), gout[j][:, :],
                                     None).then_inc(scattered[j], 16)

            pool.wait_ge(gidx_ready, 1)
            pool.wait_ge(xn_stored, 16 * BATCH)
            g.tensor_copy(gi[:, :], gidx[:, 0:RING]).then_inc(pool_step, 1)
            pool.wait_ge(pool_step, step.n + 1)
            for j in range(RING):
                g.indirect_dma_start(xg[j][:, :], None, xn_rows,
                                     bass.IndirectOffsetOnAxis(gi[:, j:j + 1], 0)).then_inc(gathered[j], 16)

            def turn(i, first=False, last=False):
                for j in range(LAST if last else RING):
                    if j % 2 == 0:
                        if not last:
                            stage_gather(i, j)
                        if j == 2:
                            stage_scatter(i, 0)
                        elif not first:
                            stage_scatter(i - 1, 2)
                    if not last:
                        gather(i, j)
                    if j >= 2:
                        scatter(i, j - 2)
                    elif not first:
                        scatter(i - 1, j + 2)

            turn(0, first=True)
            turn(1)
            with pool.Fori(2, TURNS - 1) as i:
                turn(i)
            turn(TURNS - 1, last=True)
            stage_scatter(TURNS - 1, 2)
            for j in range(LAST - 2, LAST):
                scatter(TURNS - 1, j)
            pool.wait_ge(gathered[RING - 1], 16 * TURNS)
            for c in POOL_ADDS:
                pool.wait_ge(prod_ready, c + 1)
                g.tensor_tensor(g_sb[:, c * TPB:(c + 1) * TPB, :], g_sb[:, c * TPB:(c + 1) * TPB, :],
                                x_sb[:, c * TPB:(c + 1) * TPB, :], ALU.add).then_inc(out_pool, 1)

        @block.vector
        def _(dve):
            v = nc.vector
            step = Steps(dve, dve_step)
            with_stats, normalised = [0], [0]

            def stats_tile():
                n = with_stats[0]
                with_stats[0] += 1
                if n % (NT // XLOADS) == 0:
                    dve.wait_ge(ld_x[n // (NT // XLOADS)], 16)
                return v.bn_stats(stats[:, n, :], x_sb[:, n, :])

            def finish_stats(h, go_on):
                t = slice(h * HALF, (h + 1) * HALF)
                v.tensor_tensor(msum[:, t], stats[:, t, 1], stats[:, t, 4], ALU.add)
                step.link(v.tensor_tensor(mdif[:, t], stats[:, t, 1], stats[:, t, 4], ALU.subtract))
                v.tensor_tensor(var[:, t], stats[:, t, 2], stats[:, t, 5], ALU.add)
                step.link(v.scalar_tensor_tensor(out=newt[:, t], in0=mdif[:, t], scalar=0.25, in1=mdif[:, t],
                                                 op0=ALU.mult, op1=ALU.mult), go_on)
                step.link(v.scalar_tensor_tensor(out=var[:, t], in0=var[:, t], scalar=1.0 / P, in1=newt[:, t],
                                                 op0=ALU.mult, op1=ALU.add), go_on)
                v.tensor_scalar(var[:, t], var[:, t], LN_EPS, None, ALU.add).then_inc(var_ready, 1)
                go_on()
                go_on()
                dve.wait_ge(var_ready, h + 1)
                dve.wait_ge(std_ready, h + 1)
                step.link(v.reciprocal(rstd[:, t], std[:, t]), go_on)
                step.link(v.tensor_tensor(newt[:, t], rstd[:, t], rstd[:, t], ALU.mult), go_on)
                step.link(v.tensor_tensor(newt[:, t], newt[:, t], var[:, t], ALU.mult), go_on)
                step.link(v.tensor_scalar(newt[:, t], newt[:, t], -0.5, 1.5, ALU.mult, ALU.add), go_on)
                step.link(v.tensor_tensor(rstd[:, t], rstd[:, t], newt[:, t], ALU.mult), go_on)
                v.scalar_tensor_tensor(out=nbias[:, t], in0=msum[:, t], scalar=-0.5, in1=rstd[:, t],
                                       op0=ALU.mult, op1=ALU.mult).then_inc(ln_ready, 1)
                go_on()
                dve.wait_ge(ln_ready, h + 1)

            own_tiles = [n for n in range(NT) if n % TPB >= 2]

            def normalise_tile():
                n = own_tiles[normalised[0]]
                normalised[0] += 1
                v.tensor_scalar(xn_sb[:, n, :], x_sb[:, n, :], rstd[:, n:n + 1], nbias[:, n:n + 1],
                                ALU.mult, ALU.add).then_inc(xn_dve, 1)

            def normalise_first_half():
                if normalised[0] < len(own_tiles) // 2:
                    normalise_tile()

            def mix_shifted(k):
                dve.wait_ge(mixed_a, k + 1)
                b, c = divmod(k, NBB)
                if c:
                    dve.wait_ge(xnT_ready, k + 1)
                v.scalar_tensor_tensor(out=xmT[:, k * BLK:(k + 1) * BLK], in0=xnT[:, b, c * BLK:(c + 1) * BLK],
                                       scalar=omt[:, 0:1], in1=xmT[:, k * BLK:(k + 1) * BLK],
                                       op0=ALU.mult, op1=ALU.add).then_inc(xm_ready, 1)

            while with_stats[0] < HALF:
                last = stats_tile()
            step.link(last)
            finish_stats(0, go_on=stats_tile)
            for _ in range(len(own_tiles) // 4):
                normalise_tile()
            while with_stats[0] < NT:
                last = stats_tile()
            step.link(last)
            finish_stats(1, go_on=normalise_first_half)
            dve.wait_ge(ld_small, 16 * 7)
            v.tensor_scalar(omt[:, :], tmix[:, :], -1.0, 1.0, ALU.mult, ALU.add).then_inc(omt_ready, 1)
            for k in range(NB // 2, NB):
                normalise_tile()
                normalise_tile()
                if k == NB // 2:
                    dve.wait_ge(omt_ready, 1)
                mix_shifted(k - NB // 2)
            for k in range(NB // 2, NB):
                mix_shifted(k)

            dve.wait_ge(gates, NB)
            gate_ps = psG[:, 0:NT * E].rearrange("p (n e) -> p n e", e=E)
            step.link(v.tensor_tensor(logit[:, :, :], gate_ps, bgb[:, :].unsqueeze(1).to_broadcast([P, NT, E]),
                                      ALU.add))
            step.link(v.tensor_reduce(lmax[:, :], logit[:, :, :], AX.X, ALU.max))
            step.link(v.tensor_tensor(wsel[:, :, :], logit[:, :, :],
                                      lmax[:, :].unsqueeze(2).to_broadcast([P, NT, E]), ALU.is_equal))
            step.link(v.tensor_tensor(wsel[:, :, :], wsel[:, :, :],
                                      first[:, :].unsqueeze(1).to_broadcast([P, NT, E]), ALU.mult))
            step.link(v.tensor_reduce(wmax[:, :], wsel[:, :, :], AX.X, ALU.max))
            ins = v.tensor_tensor(oh[:, :, :].rearrange("p e n -> p n e"), wsel[:, :, :],
                                  wmax[:, :].unsqueeze(2).to_broadcast([P, NT, E]), ALU.is_equal)
            ins.then_inc(oh_ready, 1)
            dve.wait_ge(oh_ready, 1)
            dve.wait_ge(prefix_ready, 1)
            EN = E * NT
            flat = lambda t: t[:, :, :].rearrange("p e n -> p (e n)")
            step.link(v.tensor_copy(flat(tot), psS[:, EN:2 * EN]))
            step.link(v.tensor_tensor_scan(flat(incl), flat(going), flat(tot), 0.0, ALU.mult, ALU.add))
            v.tensor_tensor(flat(excl), flat(incl), flat(tot), ALU.subtract)
            step.link(v.tensor_scalar(cnt_i[:, 0, :], incl[:, :, NT - 1], float(P - 1), None, ALU.add))
            step.link(v.tensor_scalar(cnt_i[:, 1, :], cnt_i[:, 0, :], 7, None, ALU.logical_shift_right))
            step.link(v.tensor_copy(tiles_f[:, :], cnt_i[:, 1, :]))
            step.link(v.tensor_tensor_scan(end_t[:, :], one8[:, :], tiles_f[:, :], 0.0, ALU.mult, ALU.add))
            step.link(v.tensor_tensor(base_s[:, :], end_t[:, :], tiles_f[:, :], ALU.subtract))
            step.link(v.tensor_scalar(base_s[:, :], base_s[:, :], float(P), None, ALU.mult))
            step.link(v.tensor_tensor(flat(posw), psS[:, 0:EN], flat(excl), ALU.add))
            step.link(v.tensor_tensor(posw[:, :, :], posw[:, :, :],
                                      base_s[:, :].unsqueeze(2).to_broadcast([P, E, NT]), ALU.add))
            step.link(v.tensor_tensor(posw[:, :, :], posw[:, :, :], oh[:, :, :], ALU.mult))
            step.link(v.tensor_reduce(pos[:, :], posw[:, :, :].rearrange("p e n -> p n e"), AX.X, ALU.add))
            step.link(v.tensor_copy(pos_i[:, 0, :], pos[:, :]))
            v.tensor_scalar(pos_i[:, 1, :], pos_i[:, 0, :], 7, None, ALU.logical_shift_right)
            step.link(v.tensor_scalar(pos_i[:, 2, :], pos_i[:, 0, :], P - 1, None, ALU.bitwise_and))
            v.tensor_copy(hi_f[:, :], pos_i[:, 1, :])
            v.tensor_copy(lo_f[:, :], pos_i[:, 2, :]).then_inc(slots_ready, 1)
            dve.wait_ge(slots_ready, 1)
            for n in range(NT - POOL_TILES):
                v.tensor_scalar(ohlo[:, n, :], iota_h[:, :], lo_f[:, n:n + 1], None, ALU.is_equal)
            dve.wait_ge(hidif_ready, 1)
            v.scalar_tensor_tensor(out=ohhi[:, :, :], in0=hidif[:, :, :], scalar=0.0,
                                   in1=tokc[:, :].unsqueeze(2).to_broadcast([P, NT, NS]),
                                   op0=ALU.is_equal, op1=ALU.mult).then_inc(onehots, 1)
            step.link(v.tensor_tensor(ecmp[:, :, :], iota_s[:, :].unsqueeze(2).to_broadcast([P, NS, E]),
                                      end_t[:, :].unsqueeze(1).to_broadcast([P, NS, E]), ALU.is_ge))
            step.link(v.tensor_reduce(esum[:, :], ecmp[:, :, :], AX.X, ALU.add))
            step.link(v.tensor_scalar(row_i[:, 1:2], row_i[:, 0:1], E - 1, None, ALU.bitwise_and))
            step.link(v.tensor_copy(row_e[:, :], row_i[:, 1:2]))
            v.tensor_scalar(sel[:, :], esum[0:BR, :], float(E - 1), row_e[:, 0:1], ALU.min, ALU.is_equal)
            v.tensor_scalar(etab[:, :], esum[:, :], float(E - 1), None, ALU.min).then_inc(experts_ready, 1)

            dve.wait_ge(inv_ps, 1)
            step.link(v.tensor_copy(inv[:, :], psG[:, 0:NS]))
            v.tensor_scalar(upper_half[:, :], inv[:, :], 0.0, None, ALU.is_gt)
            v.tensor_scalar(pad_f[:, 0, :], inv[:, :], 0.0, None, ALU.is_equal)
            step.link(v.tensor_scalar(presence[:, :], inv[:, :], 0.0, float(TOK // 2), ALU.not_equal, ALU.mult))
            step.link(v.tensor_tensor(gidx_f[:, :], inv[:, :], upper_half[:, :], ALU.subtract))
            step.link(v.tensor_tensor(gidx_f[:, :], gidx_f[:, :], presence[:, :], ALU.add))
            v.tensor_copy(gidx[:, :], gidx_f[:, :]).then_inc(gidx_ready, 1)
            step.link(v.tensor_tensor(pad_f[:, 1, :], padrow[:, :], pad_f[:, 0, :], ALU.mult))
            v.tensor_tensor(sidx[:, :], pad_f[:, 1, :], gidx_f[:, :], ALU.add).then_inc(idx_ready, 1)

            def gate_rows(i, j, reused):
                dve.wait_ge(sgm_ready, i * RING + (j + 1))
                if reused:
                    dve.wait_ge(scattered[j], i * 16)
                v.tensor_tensor(gout[j][:, :], psYe[j % 2][:, 0:P], sgm[j % 2][:, :],
                                ALU.mult).then_inc(g_ready, 1)

            def select_expert(i, j):
                return v.tensor_copy(sel_t[j][:, :], sel[:, bass.ds(i * RING + j, 1)].to_broadcast([BR, P]))

            def cap_keys(b, blocks):
                here = slice(b * T, b * T + blocks * BLK)
                dve.wait_ge(kvr_out[0], b * NBB + blocks)
                return v.tensor_scalar(kT[:, here], kT[:, here], K_CLAMP, None, ALU.min)

            def attend(i, part_no):
                q = i - 1
                here = bass.ds(q * BLK, BLK)
                n0 = step0 + q * LOOP_STEPS
                CARRY, KV, SCAN_K, SCAN_KV, NUM, RDEN_A, SIGNUM, RDEN_B = range(1, LOOP_STEPS + 1)
                half_a, half_b = slice(0, BLK // 2), slice(BLK // 2, BLK)
                decay = a[:, 0:1].to_broadcast([P, BLK])
                if part_no == 0:
                    v.tensor_scalar(z[:, :, 0:1], z[:, :, BLK:BLK + 1], keep[:, bass.ds(q, 1)], None,
                                    ALU.mult).then_inc(dve_step, 1)
                    v.tensor_tensor(vT[:, here], kT[:, here], vT[:, here], ALU.mult).then_inc(dve_step, 1)
                    dve.wait_ge(dve_step, n0 + CARRY)
                    v.tensor_tensor_scan(zk[:, 1:BLK + 1], decay, kT[:, here], zk[:, 0:1],
                                         ALU.mult, ALU.add).then_inc(dve_step, 1)
                elif part_no == 1:
                    dve.wait_ge(dve_step, n0 + KV)
                    v.tensor_tensor_scan(zkv[:, 1:BLK + 1], decay, vT[:, here], zkv[:, 0:1],
                                         ALU.mult, ALU.add).then_inc(dve_step, 1)
                    dve.wait_ge(dve_step, n0 + SCAN_K)
                    v.scalar_tensor_tensor(out=den[:, :], in0=kT[:, here], scalar=ef[:, 0:1],
                                           in1=zk[:, 0:BLK], op0=ALU.mult, op1=ALU.add).then_inc(den_ready, 1)
                    dve.wait_ge(dve_step, n0 + SCAN_KV)
                    v.scalar_tensor_tensor(out=num[:, :], in0=vT[:, here], scalar=ef[:, 0:1],
                                           in1=zkv[:, 0:BLK], op0=ALU.mult, op1=ALU.add).then_inc(dve_step, 1)
                elif part_no == 2:
                    dve.wait_ge(den_eps, i)
                    v.reciprocal(rden[:, half_a], den[:, half_a]).then_inc(dve_step, 1)
                    dve.wait_ge(dve_step, n0 + NUM)
                    dve.wait_ge(sig_ready, i)
                    v.tensor_tensor(signum[:, :], num[:, :], rT[:, here], ALU.mult).then_inc(dve_step, 1)
                elif part_no == 3:
                    v.reciprocal(rden[:, half_b], den[:, half_b]).then_inc(dve_step, 1)
                    dve.wait_ge(dve_step, n0 + SIGNUM)
                    if not isinstance(i, int):
                        dve.wait_ge(s_ps, i - 1)
                    v.tensor_tensor(rw[:, half_a], signum[:, half_a], rden[:, half_a], ALU.mult)
                else:
                    dve.wait_ge(dve_step, n0 + RDEN_B)
                    v.tensor_tensor(rw[:, half_b], signum[:, half_b], rden[:, half_b],
                                    ALU.mult).then_inc(rw_ready, 1)

            LOOP_STEPS = 8
            step0 = step.n

            def turn(i, first=False, last=False, attends=False):
                for j in range(LAST if last else RING):
                    if attends:
                        attend(i, j)
                    if j < (LAST if last else RING) - 2:
                        if not first or j:
                            select_expert(i, j + 2)
                    elif not last:
                        select_expert(i + 1, j - 2)
                    if j:
                        gate_rows(i, j - 1, reused=not first)
                    elif not first:
                        gate_rows(i - 1, RING - 1, reused=not isinstance(i, int) or i > 1)
                if attends:
                    attend(i, RING)

            cap_keys(0, NBB).then_inc(k_capped, 1)
            for k in range(ACT_BLOCKS, NB):
                here = slice(k * BLK, (k + 1) * BLK)
                dve.wait_ge(kvr_ps[0], k + 1)
                v.tensor_scalar(kT[:, here], psH0[:, :], K_CLAMP, None, ALU.min).then_inc(kvr_out[0], 1)
                if k == NB - 1:
                    cap_keys(1, ACT_BLOCKS - NBB).then_inc(k_capped, 1)
                dve.wait_ge(kvr_ps[1], k + 1)
                v.tensor_copy(vT[:, here], psH1[:, :]).then_inc(kvr_out[1], 1)
                if k == ACT_BLOCKS:
                    select_expert(0, 0)
                    select_expert(0, 1)
                    select_expert(0, 2).then_inc(sel_ready, 1)
                dve.wait_ge(kvr_ps[2], k + 1)
                v.tensor_copy(rT[:, here], psY[:, :]).then_inc(kvr_out[2], 1)
            turn(0, first=True)
            dve.wait_ge(k_ready, BATCH)
            dve.wait_ge(kvr_out[1], NB)
            dve.wait_ge(decay_ready, 1)
            turn(1, attends=True)
            with dve.Fori(2, TURNS - 1) as i:
                turn(i, attends=True)
            turn(TURNS - 1, last=True)
            gate_rows(TURNS - 1, LAST - 1, reused=True)

            dve.wait_ge(s_ready, NB)
            for c in range(NB + 1):
                if c < NB:
                    cols = slice(c * TPB, (c + 1) * TPB)
                    dve.wait_ge(g_loaded[c], 16)
                    v.tensor_tensor(g_sb[:, cols, :], g_sb[:, cols, :], s_sb[:, cols, :],
                                    ALU.mult).then_inc(prod_ready, 1)
                if c and c - 1 not in POOL_ADDS:
                    cols = slice((c - 1) * TPB, c * TPB)
                    dve.wait_ge(prod_ready, c)
                    v.tensor_tensor(g_sb[:, cols, :], g_sb[:, cols, :], x_sb[:, cols, :],
                                    ALU.add).then_inc(out_dve, 1)

        @block.scalar
        def _(act):
            s = nc.scalar
            act.dma_start(tmix[:, :], time_mix.rearrange("a b d -> d (a b)")).then_inc(ld_small, 16)
            act.dma_start(bgb[:, :], bg.rearrange("(o e) -> o e", o=1).to_broadcast([P, E])).then_inc(ld_small, 16)
            act.dma_start(wg[:, :], Wg).then_inc(ld_small, 16)
            act.dma_start(tdec[:, :], time_decay.to_broadcast([HEADS, HEAD])).then_inc(ld_small, 16)
            act.dma_start(tfir[:, :], time_first.to_broadcast([HEADS, HEAD])).then_inc(ld_small, 16)

            def deviation(h):
                t = slice(h * HALF, (h + 1) * HALF)
                act.wait_ge(var_ready, h + 1)
                s.activation(std[:, t], var[:, t], ACT.Sqrt).then_inc(std_ready, 1)

            deviation(0)
            act.wait_ge(ld_small, 16 * 7)
            for k in range(NB):
                b, c = divmod(k, NBB)
                act.wait_ge(xnT_ps, k + 1)
                s.copy(xnT[:, b, 1 + c * BLK:1 + (c + 1) * BLK], psT[k % 2][:, :]).then_inc(xnT_ready, 1)
                s.mul(xmT[:, k * BLK:(k + 1) * BLK], psT[k % 2][:, :], tmix[:, 0:1]).then_inc(mixed_a, 1)
                if k == 1:
                    deviation(1)
                if k == 3:
                    act.wait_ge(wT_ps, 1)
                    s.copy(wT[:, :, :].rearrange("p t d -> p (t d)"), psX[:, :]).then_inc(wT_ready, 1)
            s.activation(dec[:, :], tdec[:, :], ACT.Exp).then_inc(act_step, 1)
            s.activation(ef[:, :], tfir[:, :], ACT.Exp)
            act.wait_ge(act_step, 1)
            s.activation(a_exp[:, :], dec[:, :], ACT.Exp, scale=-1.0).then_inc(dec_ready, 1)

            def kvr(k):
                here = bass.ds(k * BLK, BLK)
                for t, (dst, ps) in enumerate(((kT, psH0), (vT, psH1), (rT, psY))):
                    act.wait_ge(kvr_ps[t], k + 1)
                    s.copy(dst[:, here], ps[:, :]).then_inc(kvr_out[t], 1)

            with act.Fori(0, ACT_BLOCKS) as k:
                kvr(k)

            def exp_k(b):
                act.wait_ge(k_capped, b + 1)
                s.activation(kT[:, b * T:(b + 1) * T], kT[:, b * T:(b + 1) * T], ACT.Exp).then_inc(k_ready, 1)

            def expert(i, j):
                return act.value_load(etab[0:1, bass.ds(i * RING + j, 1)], min_val=0, max_val=E - 1)

            def copy_w1(i, j):
                e = expert(i, j)
                s.copy(w1e[j % 2][:, :], w1[:, bass.ds(e, 1), :].rearrange("p o h -> p (o h)"))

            def copy_xgT(i, j):
                act.wait_ge(xgT_ps, i * RING + (j + 1))
                s.copy(xgT[j % 2][:, :], psXg[j % 2][:, 0:P]).then_inc(layer1_in, 1)

            def copy_w2(i, j):
                e = expert(i, j)
                s.copy(w2e[j % 2][:, :], w2[:, bass.ds(e * HC, HC), :].rearrange("p c d -> p (c d)"))

            def relu(i, j):
                act.wait_ge(hid_ps, i * RING + (j + 1))
                s.activation(hidT[j % 2][:, :], psH[j % 2][:, :], ACT.Relu).then_inc(hid_ready, 1)

            def sigmoid_y(i, j):
                act.wait_ge(y_ps, i * RING + (j + 1))
                if not isinstance(i, int) or i * RING + j >= 2:
                    act.wait_ge(g_ready, i * RING + (j - 1))
                s.activation(sgm[j % 2][:, :], psYe[j % 2][:, 0:P], ACT.Sigmoid).then_inc(sgm_ready, 1)

            def copy_s(i):
                act.wait_ge(s_ps, i - 1)
                s.copy(s_sb[:, bass.ds((i - 2) * TPB, TPB), :], psS[:, :].rearrange("p (n d) -> p n d", d=P)
                       ).then_inc(s_ready, 1)

            def turn(i, first=False, last=False, attends=False, projects=False):
                tiles = LAST if last else RING
                for j in range(tiles):
                    if j < tiles - 1:
                        copy_xgT(i, j + 1)
                    elif not last:
                        copy_xgT(i + 1, 0)
                    relu(i, j)
                    if j < tiles - 2:
                        copy_w1(i, j + 2)
                    elif not last:
                        copy_w1(i + 1, j - 2)
                    if attends and j == 0:
                        here = bass.ds((i - 1) * BLK, BLK)
                        s.activation(rT[:, here], rT[:, here], ACT.Sigmoid).then_inc(sig_ready, 1)
                    if attends and j == 1:
                        act.wait_ge(den_ready, i)
                        s.activation(den[:, :], den[:, :], ACT.Copy, bias=K_EPS).then_inc(den_eps, 1)
                    if projects and j == 2:
                        copy_s(i)
                    if j:
                        sigmoid_y(i, j - 1)
                    elif not first:
                        sigmoid_y(i - 1, RING - 1)
                    if j < tiles - 1:
                        copy_w2(i, j + 1)
                    elif not last:
                        copy_w2(i + 1, 0)

            act.wait_ge(experts_ready, 1)
            act.wait_ge(ld_w1, 16)
            copy_w1(0, 0)
            exp_k(0)
            copy_w1(0, 1)
            act.wait_ge(ld_w2, 16)
            copy_w2(0, 0)
            copy_xgT(0, 0)
            exp_k(1)
            act.wait_ge(inv_ps, 1)
            turn(0, first=True)
            act.wait_ge(kvr_out[2], NB)
            act.wait_ge(xn_stored, 16 * BATCH)
            turn(1, attends=True)
            with act.Fori(2, TURNS - 1) as i:
                turn(i, attends=True, projects=True)
            turn(TURNS - 1, last=True, projects=True)
            sigmoid_y(TURNS - 1, LAST - 1)

        @block.tensor
        def _(pe):
            t = nc.tensor
            pe.wait_ge(ones_ready, 1)
            for m in range(WARM_UP):
                t.matmul(psS[:, :], ones[:, :], ones[:, 0:1].to_broadcast([P, BLK]), start=True, stop=True)
            pe.wait_ge(consts, NCONST)

            def logits(k):
                b, c = divmod(k, NBB)
                pe.wait_ge(xnT_ready, k + 1)
                for j in range(TPB):
                    n = k * TPB + j
                    c0 = 1 + c * BLK + j * P
                    last = t.matmul(psG[:, n * E:(n + 1) * E], xnT[:, b, c0:c0 + P], wg[:, :],
                                    start=True, stop=True)
                last.then_inc(gates, 1)

            for k in range(NB):
                pe.wait_ge(xn_pool, k + 1)
                pe.wait_ge(xn_dve, 2 * (k + 1))
                if k >= 2:
                    pe.wait_ge(mixed_a, k - 1)
                for j in range(TPB):
                    last = t.transpose(psT[k % 2][:, j * P:(j + 1) * P], xn_sb[:, k * TPB + j, :], ident[:, :])
                last.then_inc(xnT_ps, 1)
                if k == 1:
                    pe.wait_ge(ld_small, 16 * 7)
                if k == 2:
                    pe.wait_ge(ld_proj, 16 * 4)
                    for m in range(4):
                        last = t.transpose(psX[:, m * P:(m + 1) * P], wnat[:, m, :], ident[:, :])
                    last.then_inc(wT_ps, 1)
                if k:
                    logits(k - 1)
            logits(NB - 1)

            pe.wait_ge(wT_ready, 1)

            def kvr(k, first=False, which=(0, 1, 2)):
                pe.wait_ge(xm_ready, k + 1)
                for m in which:
                    ps = (psH0, psH1, psY)[m]
                    if not first:
                        pe.wait_ge(kvr_out[m], k)
                    t.matmul(ps[:, :], wT[:, m, :], xmT[:, bass.ds(k * BLK, BLK)],
                             start=True, stop=True).then_inc(kvr_ps[m], 1)

            def prefix():
                pe.wait_ge(oh_ready, 1)
                EN = E * NT
                ohf = oh[:, :, :].rearrange("p e n -> p (e n)")
                t.matmul(psS[:, 0:EN], upper[:, :], ohf, start=True, stop=True)
                t.matmul(psS[:, EN:2 * EN], ones[:, :], ohf, start=True, stop=True).then_inc(prefix_ready, 1)

            kvr(0, first=True, which=(0, 1))
            prefix()
            kvr(0, first=True, which=(2,))
            with pe.Fori(1, NB - 3) as k:
                kvr(k)

            pe.wait_ge(onehots, 1)
            pe.wait_ge(onehots_pool, 1)
            for n in range(NT):
                last = t.matmul(psG[:, 0:NS], ohlo[:, n, :], ohhi[:, n, :], start=(n == 0), stop=(n == NT - 1))
            last.then_inc(inv_ps, 1)
            for k in range(NB - 3, NB):
                kvr(k)

            def transpose_rows(i, j):
                pe.wait_ge(gathered[j], (i + 1) * 16)
                t.transpose(psXg[j % 2][:, 0:P], xg[j][:, :], ident[:, :]).then_inc(xgT_ps, 1)

            def layer1(i, j):
                if isinstance(i, int) and i * RING + j < 3:
                    pe.wait_ge(sel_ready, 1)
                else:
                    pe.wait_ge(g_ready, i * RING + (j - 2) if j >= 2 else (i - 1) * RING + (j + 2))
                pe.wait_ge(layer1_in, i * RING + (j + 1))
                for c in range(HC):
                    cols = slice(c * P, (c + 1) * P)
                    weights = (w1e[j % 2][:, cols], xgT[j % 2][:, :])
                    bias = (bias_mat[:, cols], sel_t[j][:, :])
                    one, two = (bias, weights) if c % 2 == 0 else (weights, bias)
                    t.matmul(psH[j % 2][:, cols], *one, start=True, stop=False)
                    last = t.matmul(psH[j % 2][:, cols], *two, start=False, stop=True)
                last.then_inc(hid_ps, 1)

            def layer2(i, j):
                pe.wait_ge(hid_ready, i * RING + (j + 1))
                for c in range(HC):
                    cols = slice(c * P, (c + 1) * P)
                    t.matmul(psYe[j % 2][:, 0:P], hidT[j % 2][:, cols], w2e[j % 2][:, cols],
                             start=(c == 0), stop=False)
                t.matmul(psYe[j % 2][:, 0:P], sel_t[j][:, :], bias_mat[:, HID:],
                         start=False, stop=True).then_inc(y_ps, 1)

            def project(i):
                pe.wait_ge(rw_ready, i - 1)
                if not isinstance(i, int) or i > 2:
                    pe.wait_ge(s_ready, i - 2)
                for j in range(TPB):
                    last = t.matmul(psS[:, j * P:(j + 1) * P], rw[:, j * P:(j + 1) * P], wT[:, 3, :],
                                    start=True, stop=True)
                last.then_inc(s_ps, 1)

            def turn(i, first=False, last=False, projects=False):
                tiles = LAST if last else RING
                for j in range(tiles):
                    if j < tiles - 1:
                        transpose_rows(i, j + 1)
                    elif not last:
                        transpose_rows(i + 1, 0)
                    if first and j < 2:
                        pe.wait_ge(kvr_out[j], NB)
                    layer1(i, j)
                    if first and j == 1:
                        pe.wait_ge(kvr_out[2], NB)
                    if j:
                        layer2(i, j - 1)
                    elif not first:
                        layer2(i - 1, RING - 1)
                    if projects and j == 1:
                        project(i)

            pe.wait_ge(bias_rows_in, 16 * 6)
            transpose_rows(0, 0)
            turn(0, first=True)
            turn(1)
            turn(2, projects=True)
            with pe.Fori(3, TURNS - 1) as i:
                turn(i, projects=True)
            turn(TURNS - 1, last=True, projects=True)
            pe.wait_ge(g_ready, SLOTS - 2)
            layer2(TURNS - 1, LAST - 1)


_INS = ['L0_attn_x', 'L0_attn_time_decay', 'L0_attn_time_first', 'L0_attn_time_mix', 'L0_attn_Wk', 'L0_attn_Wv',
        'L0_attn_Wr', 'L0_attn_Wo', 'L0_ffn_Wg', 'L0_ffn_bg', 'L0_ffn_W1', 'L0_ffn_b1', 'L0_ffn_W2', 'L0_ffn_b2']


def kernel(**inputs):
    import numpy as _np
    import concourse.bacc as _bacc
    from concourse import mybir as _mybir
    from concourse.bass_utils import run_bass_kernel_spmd as _run

    nc = _bacc.Bacc("TRN2", target_bir_lowering=False, num_devices=1)
    arrays, args = {}, []
    for name in _INS:
        arr = _np.ascontiguousarray(inputs[name])
        arrays[f"in_{name}"] = arr
        args.append(nc.dram_tensor(f"in_{name}", arr.shape, _mybir.dt.from_np(arr.dtype), kind="ExternalInput").ap())
    args.append(nc.dram_tensor("out_x", (BATCH, T, P), F32, kind="ExternalOutput").ap())
    mixture_kernel(nc, *args)
    r = _run(nc, [arrays], core_ids=[0])
    return r.results[0]["out_x"]
```
